# Optimizing a Trainium2 kernel written in Bass

```python
import numpy as np
import jax
import jax.numpy as jnp

def _softmax(x, axis=-1):
    return jax.nn.softmax(x, axis=axis)

def _gelu(x):
    return jax.nn.gelu(x, approximate=True)

def _silu(x):
    return jax.nn.silu(x)

def _sigmoid(x):
    return jax.nn.sigmoid(x)

def _layernorm(x, axis=-1, eps=1e-05):
    m = jnp.mean(x, axis=axis, keepdims=True)
    v = jnp.var(x, axis=axis, keepdims=True)
    return (x - m) / jnp.sqrt(v + eps)

def _scatter_add(tgt, idx, src, axis=0):
    return tgt.at[idx].add(src)

def _segment_sum(src, seg, n):
    return jax.ops.segment_sum(src, seg, n)
kernel_name = 'mk_lm_tower_d1_tok_ids768_r4_594ae0'

def setup_inputs(seed: int=0):
    np.random.seed(seed)
    _w = jnp.asarray

    def _rec_inputs():
        import jax
        import jax.numpy as jnp
        _rk = jax.random.key(seed)
        x = jax.random.randint(jax.random.fold_in(_rk, 1), (32, 80), 0, 132540, jnp.int32)
        mask_BS_i0_1 = jnp.where(jnp.ones((32, 80), dtype=bool), 0, 1).astype(jnp.int32)
        return (x, mask_BS_i0_1)
    x, mask_BS_i0_1 = _rec_inputs()

    def _L0_tok_setup():
        import jax, jax.numpy as jnp
        import numpy as np
        WORD_LEN = 64
        KN_LEN = 64
        VOCAB = 30522
        N_ENT = 125000
        HID = 192
        MAX_POS = 128
        N_TYPES = 2
        D_ENT = 100
        B = 64
        SEQ = WORD_LEN + KN_LEN
        EPS = 1e-12

        def layer_norm(x, gamma, beta):
            u = jnp.mean(x, axis=-1, keepdims=True)
            s = jnp.mean((x - u) ** 2, axis=-1, keepdims=True)
            return gamma * (x - u) / jnp.sqrt(s + EPS) + beta

        def _compact_row(row_id, row_tt):
            wmask = (row_id > 0) & (row_id < VOCAB)
            worder = jnp.argsort(jnp.logical_not(wmask), stable=True)[:WORD_LEN]
            wvalid = jnp.arange(WORD_LEN) < jnp.sum(wmask)
            wid = jnp.where(wvalid, row_id[worder], 0)
            wtt = jnp.where(wvalid, row_tt[worder], 1)
            wpos = jnp.where(wvalid, worder, jnp.arange(WORD_LEN))
            kmask = row_id >= VOCAB
            korder = jnp.argsort(jnp.logical_not(kmask), stable=True)[:KN_LEN]
            kvalid = jnp.arange(KN_LEN) < jnp.sum(kmask)
            kid = jnp.where(kvalid, row_id[korder] - VOCAB, 0)
            ktt = jnp.where(kvalid, row_tt[korder], 0)
            kpos = jnp.where(kvalid, korder, 0)
            return (wid, wtt, wpos, kid, ktt, kpos, kvalid)
        key = jax.random.key(seed)
        ks = jax.random.split(key, 16)
        wpart = jax.random.randint(ks[0], (B, WORD_LEN), 1, VOCAB, dtype=jnp.int32)
        wpart = jnp.where(jax.random.uniform(ks[1], (B, WORD_LEN)) < 0.9, wpart, 0)
        kpart = jax.random.randint(ks[2], (B, KN_LEN), VOCAB, VOCAB + N_ENT, dtype=jnp.int32)
        kpart = jnp.where(jax.random.uniform(ks[3], (B, KN_LEN)) < 0.5, kpart, 0)
        ids = jnp.concatenate([wpart, kpart], axis=1)
        perm = jax.vmap(lambda k: jax.random.permutation(k, SEQ))(jax.random.split(ks[4], B))
        input_ids = jnp.take_along_axis(ids, perm, axis=1)
        token_type_ids = jax.random.randint(ks[5], (B, SEQ), 0, N_TYPES, dtype=jnp.int32)
        return {'input_ids': input_ids, 'token_type_ids': token_type_ids, 'word_emb': 0.02 * jax.random.normal(ks[6], (VOCAB, HID), jnp.float32), 'pos_emb': 0.02 * jax.random.normal(ks[7], (MAX_POS, HID), jnp.float32), 'tt_emb': 0.02 * jax.random.normal(ks[8], (N_TYPES, HID), jnp.float32), 'entityVec': jax.random.normal(ks[9], (N_ENT, D_ENT), jnp.float32), 'ke_w': 0.02 * jax.random.normal(ks[10], (HID, D_ENT), jnp.float32), 'ke_b': 0.02 * jax.random.normal(ks[11], (HID,), jnp.float32), 'w_gamma': 1.0 + 0.1 * jax.random.normal(ks[12], (HID,), jnp.float32), 'w_beta': 0.1 * jax.random.normal(ks[13], (HID,), jnp.float32), 'k_gamma': 1.0 + 0.1 * jax.random.normal(ks[14], (HID,), jnp.float32), 'k_beta': 0.1 * jax.random.normal(ks[15], (HID,), jnp.float32)}
    _L0_tok_all = _L0_tok_setup()
    _L0_tok_in = {k: v for k, v in _L0_tok_all.items() if k in ('word_emb', 'pos_emb', 'tt_emb', 'entityVec', 'ke_w', 'ke_b', 'w_gamma', 'w_beta', 'k_gamma', 'k_beta')}
    del _L0_tok_all

    def _L0_attn_setup():
        import jax, jax.numpy as jnp
        import numpy as np
        HIDDEN = 192
        HEADS = 8
        key = jax.random.key(seed)
        ks = jax.random.split(key, 5)
        b, n = (2, 256)
        x = jax.random.normal(ks[0], (b, n, HIDDEN), dtype=jnp.float32)
        W_qkv = jax.random.normal(ks[1], (HIDDEN, 3 * HIDDEN * HEADS), dtype=jnp.float32) * 0.02
        b_qkv = jnp.zeros((3 * HIDDEN * HEADS,), dtype=jnp.float32)
        W_proj = jax.random.normal(ks[2], (HEADS * HIDDEN, HIDDEN), dtype=jnp.float32) * 0.02
        b_proj = jnp.zeros((HIDDEN,), dtype=jnp.float32)
        return {'x': x, 'W_qkv': W_qkv, 'b_qkv': b_qkv, 'W_proj': W_proj, 'b_proj': b_proj}
    _L0_attn_all = _L0_attn_setup()
    _L0_attn_in = {k: v for k, v in _L0_attn_all.items() if k in ('W_qkv', 'b_qkv', 'W_proj', 'b_proj')}
    del _L0_attn_all

    def _L0_ffn_setup():
        import jax, jax.numpy as jnp
        import numpy as np
        NHEAD = 12
        EPS_Z = 1e-05
        EPS_LN = 1e-05

        def _zscore_last(t, n):
            m = t.mean(axis=-1, keepdims=True)
            var = ((t - m) ** 2).sum(axis=-1, keepdims=True) / (n - 1)
            return (t - m) / (jnp.sqrt(var) + EPS_Z)

        def _layernorm(x, g, b):
            m = x.mean(axis=-1, keepdims=True)
            v = ((x - m) ** 2).mean(axis=-1, keepdims=True)
            return (x - m) * jax.lax.rsqrt(v + EPS_LN) * g + b
        key = jax.random.key(seed)
        ks = jax.random.split(key, 20)
        B, T, D, FF, E = (2, 256, 192, 768, 4)
        p = lambda k, shape: jax.random.normal(k, shape, jnp.float32) * 0.02
        return {'src': jax.random.normal(ks[0], (B, T, D), jnp.float32), 'frac': jax.random.uniform(ks[1], (B, T), jnp.float32), 'Wq': p(ks[2], (D, D)), 'bq': jnp.zeros((D,), jnp.float32), 'Wk': p(ks[3], (D, D)), 'bk': jnp.zeros((D,), jnp.float32), 'Wv': p(ks[4], (D, D)), 'bv': jnp.zeros((D,), jnp.float32), 'Wo': p(ks[5], (D, D)), 'bo': jnp.zeros((D,), jnp.float32), 'gamma': jnp.float32(1.0), 'ln1_g': jnp.ones((D,), jnp.float32), 'ln1_b': jnp.zeros((D,), jnp.float32), 'ln2_g': jnp.ones((D,), jnp.float32), 'ln2_b': jnp.zeros((D,), jnp.float32), 'Wg': p(ks[6], (E, D)), 'bg': jnp.zeros((E,), jnp.float32), 'W1': p(ks[7], (E, D, FF)), 'b1': jnp.zeros((E, FF), jnp.float32), 'W2': p(ks[8], (E, FF, D)), 'b2': jnp.zeros((E, D), jnp.float32)}
    _L0_ffn_all = _L0_ffn_setup()
    _L0_ffn_in = {k: v for k, v in _L0_ffn_all.items() if k in ('frac', 'Wq', 'bq', 'Wk', 'bk', 'Wv', 'bv', 'Wo', 'bo', 'gamma', 'ln1_g', 'ln1_b', 'ln2_g', 'ln2_b', 'Wg', 'bg', 'W1', 'b1', 'W2', 'b2')}
    del _L0_ffn_all
    return {'x': x, 'mask_BS_i0_1': mask_BS_i0_1, 'L0_tok_word_emb': _L0_tok_in['word_emb'], 'L0_tok_pos_emb': _L0_tok_in['pos_emb'], 'L0_tok_tt_emb': _L0_tok_in['tt_emb'], 'L0_tok_entityVec': _L0_tok_in['entityVec'], 'L0_tok_ke_w': _L0_tok_in['ke_w'], 'L0_tok_ke_b': _L0_tok_in['ke_b'], 'L0_tok_w_gamma': _L0_tok_in['w_gamma'], 'L0_tok_w_beta': _L0_tok_in['w_beta'], 'L0_tok_k_gamma': _L0_tok_in['k_gamma'], 'L0_tok_k_beta': _L0_tok_in['k_beta'], 'L0_attn_W_qkv': _L0_attn_in['W_qkv'], 'L0_attn_b_qkv': _L0_attn_in['b_qkv'], 'L0_attn_W_proj': _L0_attn_in['W_proj'], 'L0_attn_b_proj': _L0_attn_in['b_proj'], 'L0_ffn_frac': _L0_ffn_in['frac'], 'L0_ffn_Wq': _L0_ffn_in['Wq'], 'L0_ffn_bq': _L0_ffn_in['bq'], 'L0_ffn_Wk': _L0_ffn_in['Wk'], 'L0_ffn_bk': _L0_ffn_in['bk'], 'L0_ffn_Wv': _L0_ffn_in['Wv'], 'L0_ffn_bv': _L0_ffn_in['bv'], 'L0_ffn_Wo': _L0_ffn_in['Wo'], 'L0_ffn_bo': _L0_ffn_in['bo'], 'L0_ffn_gamma': _L0_ffn_in['gamma'], 'L0_ffn_ln1_g': _L0_ffn_in['ln1_g'], 'L0_ffn_ln1_b': _L0_ffn_in['ln1_b'], 'L0_ffn_ln2_g': _L0_ffn_in['ln2_g'], 'L0_ffn_ln2_b': _L0_ffn_in['ln2_b'], 'L0_ffn_Wg': _L0_ffn_in['Wg'], 'L0_ffn_bg': _L0_ffn_in['bg'], 'L0_ffn_W1': _L0_ffn_in['W1'], 'L0_ffn_b1': _L0_ffn_in['b1'], 'L0_ffn_W2': _L0_ffn_in['W2'], 'L0_ffn_b2': _L0_ffn_in['b2']}

def reference(x, mask_BS_i0_1, L0_tok_word_emb, L0_tok_pos_emb, L0_tok_tt_emb, L0_tok_entityVec, L0_tok_ke_w, L0_tok_ke_b, L0_tok_w_gamma, L0_tok_w_beta, L0_tok_k_gamma, L0_tok_k_beta, L0_attn_W_qkv, L0_attn_b_qkv, L0_attn_W_proj, L0_attn_b_proj, L0_ffn_frac, L0_ffn_Wq, L0_ffn_bq, L0_ffn_Wk, L0_ffn_bk, L0_ffn_Wv, L0_ffn_bv, L0_ffn_Wo, L0_ffn_bo, L0_ffn_gamma, L0_ffn_ln1_g, L0_ffn_ln1_b, L0_ffn_ln2_g, L0_ffn_ln2_b, L0_ffn_Wg, L0_ffn_bg, L0_ffn_W1, L0_ffn_b1, L0_ffn_W2, L0_ffn_b2):
    import jax
    import jax.numpy as jnp

    def _L0_tok_ref(input_ids, token_type_ids, word_emb, pos_emb, tt_emb, entityVec, ke_w, ke_b, w_gamma, w_beta, k_gamma, k_beta):
        import jax, jax.numpy as jnp
        import numpy as np
        WORD_LEN = 64
        KN_LEN = 64
        VOCAB = 30522
        N_ENT = 125000
        HID = 192
        MAX_POS = 128
        N_TYPES = 2
        D_ENT = 100
        B = 64
        SEQ = WORD_LEN + KN_LEN
        EPS = 1e-12

        def layer_norm(x, gamma, beta):
            u = jnp.mean(x, axis=-1, keepdims=True)
            s = jnp.mean((x - u) ** 2, axis=-1, keepdims=True)
            return gamma * (x - u) / jnp.sqrt(s + EPS) + beta

        def _compact_row(row_id, row_tt):
            wmask = (row_id > 0) & (row_id < VOCAB)
            worder = jnp.argsort(jnp.logical_not(wmask), stable=True)[:WORD_LEN]
            wvalid = jnp.arange(WORD_LEN) < jnp.sum(wmask)
            wid = jnp.where(wvalid, row_id[worder], 0)
            wtt = jnp.where(wvalid, row_tt[worder], 1)
            wpos = jnp.where(wvalid, worder, jnp.arange(WORD_LEN))
            kmask = row_id >= VOCAB
            korder = jnp.argsort(jnp.logical_not(kmask), stable=True)[:KN_LEN]
            kvalid = jnp.arange(KN_LEN) < jnp.sum(kmask)
            kid = jnp.where(kvalid, row_id[korder] - VOCAB, 0)
            ktt = jnp.where(kvalid, row_tt[korder], 0)
            kpos = jnp.where(kvalid, korder, 0)
            return (wid, wtt, wpos, kid, ktt, kpos, kvalid)
        wid, wtt, wpos, kid, ktt, kpos, kvalid = jax.vmap(_compact_row)(input_ids, token_type_ids)
        word = word_emb[wid] + tt_emb[wtt] + pos_emb[wpos]
        word = layer_norm(word, w_gamma, w_beta)
        ev = jnp.where(kvalid[..., None], entityVec[kid], 0.0)
        kn = jnp.einsum('bke,he->bkh', ev, ke_w) + ke_b + tt_emb[ktt] + pos_emb[kpos]
        kn = kn * kvalid[..., None].astype(kn.dtype)
        kn = layer_norm(kn, k_gamma, k_beta)
        return jnp.concatenate([word, kn], axis=1)

    def _L0_attn_ref(x, W_qkv, b_qkv, W_proj, b_proj):
        import jax, jax.numpy as jnp
        import numpy as np
        HIDDEN = 192
        HEADS = 8
        b, n, c = x.shape
        qkv = x @ W_qkv + b_qkv
        q, k, v = jnp.split(qkv, 3, axis=-1)
        q = q.reshape(b, HEADS, n, HIDDEN)
        k = k.reshape(b, HEADS, n, HIDDEN)
        v = v.reshape(b, HEADS, n, HIDDEN)
        energy = jnp.einsum('bhqd,bhkd->bhqk', q, k)
        scaling = jnp.float32(HIDDEN ** 0.5)
        attn = jax.nn.softmax(energy, axis=-1) / scaling
        out = jnp.einsum('bhal,bhlv->bhav', attn, v)
        out = out.reshape(b, n, HEADS * HIDDEN)
        return out @ W_proj + b_proj

    def _L0_ffn_ref(src, frac, Wq, bq, Wk, bk, Wv, bv, Wo, bo, gamma, ln1_g, ln1_b, ln2_g, ln2_b, Wg, bg, W1, b1, W2, b2):
        import jax, jax.numpy as jnp
        import numpy as np
        NHEAD = 12
        EPS_Z = 1e-05
        EPS_LN = 1e-05

        def _zscore_last(t, n):
            m = t.mean(axis=-1, keepdims=True)
            var = ((t - m) ** 2).sum(axis=-1, keepdims=True) / (n - 1)
            return (t - m) / (jnp.sqrt(var) + EPS_Z)

        def _layernorm(x, g, b):
            m = x.mean(axis=-1, keepdims=True)
            v = ((x - m) ** 2).mean(axis=-1, keepdims=True)
            return (x - m) * jax.lax.rsqrt(v + EPS_LN) * g + b
        B, T, D = src.shape
        H = NHEAD
        hd = D // H
        scale = hd ** (-0.5)
        Q = (src @ Wq.T + bq).reshape(B, T, H, hd)
        K = (src @ Wk.T + bk).reshape(B, T, H, hd)
        V = (src @ Wv.T + bv).reshape(B, T, H, hd)
        logits = jnp.einsum('bqhd,bkhd->bhqk', Q, K) * scale
        logits = gamma * _zscore_last(logits, T)
        probs = jax.nn.softmax(logits, axis=-1)
        attn = jnp.einsum('bhqk,bkhd->bqhd', probs, V).reshape(B, T, D)
        attn = attn @ Wo.T + bo
        x = _layernorm(src + attn, ln1_g, ln1_b)
        E = Wg.shape[0]
        gate_scores = jax.nn.softmax(x @ Wg.T + bg, axis=-1)
        top2_val, top2_idx = jax.lax.top_k(gate_scores, 2)
        combine = (jax.nn.one_hot(top2_idx, E, dtype=x.dtype) * top2_val[..., None]).sum(axis=-2)
        h = jax.nn.relu(jnp.einsum('btd,edf->ebtf', x, W1) + b1[:, None, None, :])
        y = jnp.einsum('ebtf,efd->ebtd', h, W2) + b2[:, None, None, :]
        ff = jnp.einsum('ebtd,bte->btd', y, combine)
        return _layernorm(x + ff, ln2_g, ln2_b)
    h = _L0_tok_ref(x, mask_BS_i0_1, L0_tok_word_emb, L0_tok_pos_emb, L0_tok_tt_emb, L0_tok_entityVec, L0_tok_ke_w, L0_tok_ke_b, L0_tok_w_gamma, L0_tok_w_beta, L0_tok_k_gamma, L0_tok_k_beta)
    h = h + _L0_attn_ref(_layernorm(h, axis=-1), L0_attn_W_qkv, L0_attn_b_qkv, L0_attn_W_proj, L0_attn_b_proj)
    h = h + _L0_ffn_ref(_layernorm(h, axis=-1), L0_ffn_frac, L0_ffn_Wq, L0_ffn_bq, L0_ffn_Wk, L0_ffn_bk, L0_ffn_Wv, L0_ffn_bv, L0_ffn_Wo, L0_ffn_bo, L0_ffn_gamma, L0_ffn_ln1_g, L0_ffn_ln1_b, L0_ffn_ln2_g, L0_ffn_ln2_b, L0_ffn_Wg, L0_ffn_bg, L0_ffn_W1, L0_ffn_b1, L0_ffn_W2, L0_ffn_b2)
    return h

_drawn_inputs = setup_inputs


def setup_inputs(seed=0):
    import zlib

    import numpy as np

    out = dict(_drawn_inputs(seed))
    spreads = {'L0_attn_b_qkv': (0.0, 0.8),
     'L0_attn_b_proj': (0.0, 0.1),
     'L0_ffn_bq': (0.0, 2.0),
     'L0_ffn_bk': (0.0, 2.0),
     'L0_ffn_bv': (0.0, 0.58),
     'L0_ffn_bo': (0.0, 0.1),
     'L0_ffn_ln1_g': (1.0, 0.2),
     'L0_ffn_ln1_b': (0.0, 0.1),
     'L0_ffn_ln2_g': (1.0, 0.2),
     'L0_ffn_ln2_b': (0.0, 0.1),
     'L0_ffn_bg': (0.0, 0.8),
     'L0_ffn_b1': (0.0, 0.79),
     'L0_ffn_b2': (0.0, 0.299)}
    factors = {'L0_attn_W_qkv': 8.0,
     'L0_attn_W_proj': 8.0,
     'L0_ffn_Wq': 8.0,
     'L0_ffn_Wk': 8.0,
     'L0_ffn_Wv': 3.711,
     'L0_ffn_Wo': 2.758}
    for name, (base, spread) in spreads.items():
        noise = np.random.default_rng([zlib.crc32(name.encode()), seed]).standard_normal(out[name].shape)
        drawn = base * np.exp(spread * noise) if base else spread * noise
        out[name] = jnp.asarray(drawn.astype(out[name].dtype))
    for name, factor in factors.items():
        out[name] = (out[name] * factor).astype(out[name].dtype)
    return out
```

```python
import concourse.bass as bass
from concourse import mybir
from contextlib import ExitStack

B, S = 32, 80
HALF = 64
T = 2 * HALF
VOCAB, N_ENT, D_ENT = 30522, 125000, 100
D = 192
HEADS = 8
FHEADS, HD = 12, 16
E, FF = 4, 768
EPS_TOK, EPS = 1e-12, 1e-5

P = 128
R = D - P
PAIRS = B // 2
NT = 2 * T
HP = HEADS // 2
QCH = 3 * HP
GT = T // HEADS
FCH = FHEADS // 4
FU = 2 * 4
KCH = FF // P
XW = D + 2

UP = [f"up{n}" for n in range(E * KCH // 2)]
QU, KU = ([f"{k}{n}" for n in range(QCH // 2)] for k in "qk")
VU = [f"v{n}" for n in range(6)]
OU = ["om0", "om1", "or0", "om2", "om3", "or1"]
DRAINS = {
    "ids": ["ids", "prefix", "ke_w"],
    "first": ["index", "ent", "proj", "small", "fq", "fk", "fv", "fo", "aT", *VU, *QU],
    "peel": [*KU[:3], "index", *KU[3:], *OU, "ent", "bT", "proj", "qk0", "qk1", "qk2", "fval", "aT", *VU, *QU],
    "loop": [*KU[:3], "attnT", *KU[3:], "wo", "index", *OU, "xT", "ent", *UP[:3], "proj", *UP[3:6], "bT",
             *UP[6:], "aT", "qk0", "qk1", "qk2", "fval", *VU, *QU],
    "final": [*KU[:3], "attnT", *KU[3:], "wo", *OU, "xT", *UP[:6], "bT", *UP[6:], "qk0", "qk1", "qk2", "fval"],
    "last": ["attnT", "wo", "xT", *UP],
}
SUMS = {
    "peel": ["attn", "ffn"],
    "loop": ["attn", "y0", "y1", "y2", "y3", "ffn"],
    "final": ["attn", "y0", "y1", "y2", "y3", "ffn"],
    "last": ["y0", "y1", "y2", "y3"],
}
TURNS = {"ids": 1, "first": 1, "peel": 1, "loop": PAIRS - 2, "final": 1, "last": 1}


def numbered(orders):
    start, n = {}, 0
    for part, turns in TURNS.items():
        start[part] = n
        n += turns * len(orders.get(part, []))
    return start


DRAIN_START, SUM_START = numbered(DRAINS), numbered(SUMS)


def drain_no(at, name):
    part, turn = at
    return turn * len(DRAINS[part]) + DRAIN_START[part] + DRAINS[part].index(name)


def sum_no(at, name):
    part, turn = at
    return turn * len(SUMS[part]) + SUM_START[part] + SUMS[part].index(name)


class Steps:

    def __init__(self, eng, sem, turn, per):
        self.eng, self.sem, self.base, self.per, self.n = eng, sem, turn * per, per, 0

    def did(self, ins):
        self.n += 1
        ins.then_inc(self.sem, 1)

    def wait(self):
        self.eng.wait_ge(self.sem, self.base + self.n)

    def end(self):
        assert self.n == self.per, (self.sem, self.n, self.per)


def lm_tower_kernel(nc, x, mask, word_emb, pos_emb, tt_emb, ent_emb, ke_w, ke_b, w_gamma, w_beta, k_gamma, k_beta,
                    W_qkv, b_qkv, W_proj, b_proj, Wq, bq, Wk, bk, Wv, bv, Wo, bo, gamma, ln1_g, ln1_b,
                    ln2_g, ln2_b, Wg, bg, W1, b1, W2, b2, out):
    f32, f32r, i32 = mybir.dt.float32, mybir.dt.float32r, mybir.dt.int32
    ALU, ACT, AX = mybir.AluOpType, mybir.ActivationFunctionType, mybir.AxisListType
    ds = bass.ds

    with ExitStack() as ctx:
        def sb(name, shape, dt=f32):
            return ctx.enter_context(nc.sbuf_tensor(name, shape, dt))

        def sem(name):
            return ctx.enter_context(nc.semaphore(name))

        wq, wk, wv = (sb(n, [P, HEADS * D]) for n in ("wq", "wk", "wv"))
        wqkR = sb("wqkR", [P, HEADS * D])
        wvR = sb("wvR", [P, 2 * 512])
        wp, wpR = sb("wp", [P, HEADS, D]), sb("wpR", [P, HP, D])
        bv2 = sb("bv2", [P, D])
        w1H, w1L, w1S = (sb(f"w1{k}", [P, E * FF], f32r) for k in "HLS")
        w2 = sb("w2", [P, E * KCH, D])
        fqH, fqL, fqS = (sb(f"fq{k}", [P, FCH * P], f32r) for k in "HLS")
        fkH, fkL, fkS = (sb(f"fk{k}", [P, FCH * P], f32r) for k in "HLS")
        fvo = sb("fvo", [P, 2, 2 * D])
        kewT = sb("kewT", [D_ENT, D])
        wgT = sb("wgT", [P, 2 * E])
        b1c = sb("b1c", [P, E * KCH])
        qkbias = sb("qkbias", [P, 2 * QCH])
        fqb, fkb = sb("fqb", [P, FCH]), sb("fkb", [P, FCH])
        qscale, gabs = sb("qscale", [P, 1]), sb("gabs", [P, 1])
        gam, bet = sb("gam", [P, D]), sb("bet", [P, D])
        obias, boB, bvB = sb("obias", [P, D]), sb("boB", [P, D]), sb("bvB", [P, D])
        g1, be1, g2, be2 = (sb(n, [P, D]) for n in ("g1", "be1", "g2", "be2"))
        bgB, b2B = sb("bgB", [P, E]), sb("b2B", [P, E, D])
        slotC = sb("slotC", [P, D])
        ident, ones, iota = sb("ident", [P, P]), sb("ones", [P, P]), sb("iota", [S, T])
        upper = sb("upper", [S, S])
        earlier = sb("earlier", [P, E, E])
        sgn, off = sb("sgn", [P, 1]), sb("off", [P, 1])
        mhalf, half = sb("mhalf", [P, 2]), sb("half", [P, 2 * FCH])
        ids_i = sb("ids_i", [B, 2, S], i32)
        ids_f = sb("ids_f", [B, 2, S])
        idT = sb("idT", [S, 2, B])
        kmask, slot, val, ttv = sb("kmask", [S, 2, B]), sb("slot", [S, B + 2]), sb("val", [S, B + 2]), sb("ttv", [S, B + 2])
        pref = sb("pref", [S, 2, B])
        post, ttd, tt0 = sb("post", [S, D]), sb("ttd", [S, D]), sb("tt0", [S, D])
        onehot, embR = sb("onehot", [S, 2, T]), sb("embR", [S, 2, XW])
        emb = sb("emb", [P, 2, XW])
        idxw, idxk = sb("idxw", [HALF, 2], i32), sb("idxk", [P, 1], i32)
        rows = sb("rows", [P, 2, D])
        entg, entT = sb("entg", [P, D_ENT]), sb("entT", [D_ENT, P])
        coef = sb("coef", [P, 2])
        h0, h1, h1keep = (sb(n, [P, 2, D]) for n in ("h0", "h1", "h1keep"))
        bD, xD = (sb(n, [P, 2, 2 * P]) for n in ("bD", "xD"))
        aD = xD
        bT, xT = (sb(n, [P, 2 * NT]) for n in ("bT", "xT"))
        aT = xT
        xH, xL = (sb(n, [P, 2 * NT], f32r) for n in ("xH", "xL"))
        bH, bL = xH, xL
        qt, kt = sb("qt", [P, QCH * NT]), sb("kt", [P, QCH * NT])
        NM, NR = HEADS * NT, HEADS * T
        hid = qt[:, :].rearrange("p (a k n) -> p a k n", a=2, k=KCH)
        vp = sb("vp", [P, 2, HEADS * D])
        v2 = sb("v2", [P, 2 * HEADS, D])
        oflat = vp[:, :, :].rearrange("p s n -> p (s n)")
        oT = oflat[:, 0:NM].rearrange("p (c n) -> p c n", c=HEADS)
        oR = oflat[:, NM:NM + NR].rearrange("p (c n) -> p c n", c=HP)
        prob = sb("prob", [P, 4, 4, T])
        probT = sb("probT", [P, 2, 4, T])
        fqT, fkT = (kt[:, k * FCH * NT:(k + 1) * FCH * NT].rearrange("p (c n) -> p c n", c=FCH) for k in range(2))
        fval = sb("fval", [P, 2, D])
        fo, foT, fwo, pre = sb("fo", [P, 2, D]), sb("foT", [P, 2, NT]), sb("fwo", [P, 2, D]), sb("pre", [P, 2, D])
        ff, res = pre, sb("res", [P, 2, D])
        st, mv, ve, rstd = sb("st", [P, 2, 6]), sb("mv", [P, 2, 2]), sb("ve", [P, 2]), sb("rstd", [P, 2])
        nmax, asum, arec = sb("nmax", [P, 4, 4]), sb("asum", [P, 4, 4]), sb("arec", [P, 4, 4])
        fst = sb("fst", [P, 2 * FCH, 6])
        fmax, fd, fw, fm2, fvar, fsd = (sb(n, [P, 2 * FCH]) for n in ("fmax", "fd", "fw", "fm2", "fvar", "fsd"))
        fden, finv, fsc, fnb = (sb(n, [P, 4, 2 * FCH]) for n in ("fden", "finv", "fsc", "fnb"))
        fsum, frec = sb("fsum", [P, 2, FHEADS]), sb("frec", [P, 2, FHEADS])
        gl, gs, gx, gp, grk, comb = (sb(n, [P, 2, E]) for n in ("gl", "gs", "gx", "gp", "grk", "comb"))
        gm, gsum, grec = sb("gm", [P, 2]), sb("gsum", [P, 2]), sb("grec", [P, 2])
        ggt, gge = sb("ggt", [P, 2, E, E]), sb("gge", [P, 2, E, E])
        def part(t, start, rows_, *dims):
            flat = t if len(t.shape) == 2 else t.rearrange("p a b -> p (a b)") if len(t.shape) == 3 else \
                t.rearrange("p a b c -> p (a b c)")
            n = 1
            for d in dims:
                n *= d
            v = flat[0:rows_, start:start + n]
            return v if len(dims) == 1 else v.rearrange("p (a b) -> p a b", a=dims[0])

        brow = part(probT[:, :, :, :], 0, 2 * QCH, P)
        fstage = part(prob[:, :, :, :], 0, P, 8 * D)
        kwA, kwB = part(prob[:, :, :, :], 8 * D, P, D_ENT), part(prob[:, :, :, :], 8 * D + D_ENT, R, D_ENT)
        b1row = part(prob[:, :, :, :], 8 * D + 2 * D_ENT, E * KCH, P)
        fqk = (part(probT[:, :, :, :], P, P, 2 * D), part(probT[:, :, :, :], P + 2 * D, P, 2 * D), fvo[:, 0, :], fvo[:, 1, :])
        wgrow = part(h1[:, :, :], 0, E, D)
        w1A, w1B = qt[:, :], vp[0:R, :, :].rearrange("p s n -> p (s n)")
        gsc = sb("gsc", [P, 1])

        unit = [ctx.enter_context(nc.psum_tensor(f"unit{n}", [P, 4, T], f32)) for n in range(4)]
        bank = [ctx.enter_context(nc.psum_tensor(f"bank{n}", [P, 512], f32)) for n in range(3)]
        acc = ctx.enter_context(nc.psum_tensor("acc", [P, 512], f32))

        def place(at, name):
            return bank[DRAINS[at[0]].index(name) % 3]

        def unit_of(n):
            return unit[n % 4]

        filled, drained = sem("filled"), sem("drained")
        acc_filled, acc_drained = sem("acc_filled"), sem("acc_drained")
        ld_ids, ld_tok, ld_small, ld_w1, ld_w2 = sem("ld_ids"), sem("ld_tok"), sem("ld_small"), sem("ld_w1"), sem("ld_w2")
        ld_attn, v_moved, v_ready = sem("ld_attn"), (sem("v_moved0"), sem("v_moved1")), sem("v_ready")
        stats_seen = sem("stats_seen")
        zeroed, const_ready = sem("zeroed"), sem("const_ready")
        ids_ready, mask_ready, table_ready, pro_ready = sem("ids_ready"), sem("mask_ready"), sem("table_ready"), sem("pro_ready")
        w1_hi, w1_split = sem("w1_hi"), sem("w1_split")
        pro_step = sem("pro_step")
        onehot_ready, idx_ready, gather_go, got_words, got_ents = (sem(n) for n in ("onehot_ready", "idx_ready", "gather_go", "got_words", "got_ents"))
        index_step, tok_step, attn_step, ftail_step, moe_step, ffn_step = (
            sem(n) for n in ("index_step", "tok_step", "attn_step", "ftail_step", "moe_step", "ffn_step"))
        var_ready = {k: sem(f"var_{k}") for k in "tabxo"}
        rstd_ready = {k: sem(f"rstd_{k}") for k in "tabxo"}
        aD_ready, bD_ready, xD_ready = sem("aD_ready"), sem("bD_ready"), sem("xD_ready")
        b_split, x_split = sem("b_split"), sem("x_split")
        a_scores, a_max, a_exp, a_prob, a_turned, a_probT = (sem(n) for n in ("a_scores", "a_max", "a_exp", "a_prob", "a_turned", "a_probT"))
        f_scores, f_var, f_sd, f_scale, f_exp, f_turned, f_probT = (
            sem(n) for n in ("f_scores", "f_var", "f_sd", "f_scale", "f_exp", "f_turned", "f_probT"))
        fval_ready, fo_ready = sem("fval_ready"), sem("fo_ready")
        gate_ready, gate_shift, gate_exp = sem("gate_ready"), sem("gate_shift"), sem("gate_exp")
        out_ready, stored = sem("out_ready"), sem("stored")

        block = ctx.enter_context(nc.Block())

        TOK, SMALL = 13, 32

        @block.sync
        def _(sp):
            def tok(dst, src):
                sp.dma_start(dst, src).then_inc(ld_tok, 16)

            def row(dst, src):
                sp.dma_start(dst, src).then_inc(ld_small, 16)

            def bcast(dst, src):
                row(dst, src[None, :].to_broadcast([P, src.shape[0]]))

            def load(dst, src):
                sp.dma_start(dst, src).then_inc(ld_attn, 16)

            def load_blocks(dst, src):
                dst = dst.rearrange("r (p n) -> r p n", p=HP)
                src = src.rearrange("r (p j n) -> r p j n", j=2, n=D)
                load(dst[:, :, 0:D], src[:, :, 0, :])
                load(dst[:, :, D:2 * P], src[:, :, 1, P:D])
                load(dst[:, :, 2 * P:3 * P], src[:, :, 1, 0:P])

            sp.dma_start(ids_i[:, 0, :], x).then_inc(ld_ids, 16)
            sp.dma_start(ids_i[:, 1, :], mask).then_inc(ld_ids, 16)
            tok(kwA[:, :], ke_w[0:P, :])
            tok(kwB[:, :], ke_w[P:D, :])
            tok(post[:, :], pos_emb[0:S, :])
            tok(tt0[:, :], tt_emb[0:1, :].to_broadcast([S, D]))
            tok(ttd[:, :], tt_emb[1:2, :].to_broadcast([S, D]))
            tok(slotC[0:HALF, :], pos_emb[0:HALF, :])
            tok(slotC[HALF:P, :], ke_b[None, :].to_broadcast([HALF, D]))
            tok(rows[0:HALF, 0, :], tt_emb[1:2, :].to_broadcast([HALF, D]))
            for lo, g, b in ((0, w_gamma, w_beta), (HALF, k_gamma, k_beta)):
                tok(gam[lo:lo + HALF, :], g[None, :].to_broadcast([HALF, D]))
                tok(bet[lo:lo + HALF, :], b[None, :].to_broadcast([HALF, D]))
            tok(obias[:, :], b_proj[None, :].to_broadcast([P, D]))
            sp.dma_start(w1A.rearrange("p (e n) -> p e n", e=E), W1[:, 0:P, :].rearrange("e k n -> k e n")).then_inc(ld_w1, 16)
            sp.dma_start(w1B.rearrange("p (e n) -> p e n", e=E), W1[:, P:D, :].rearrange("e k n -> k e n")).then_inc(ld_w1, 16)
            w = [W_qkv[:, m * HEADS * D:(m + 1) * HEADS * D] for m in range(3)]
            load(wv[:, :], w[2][0:P, :])
            load(wvR[0:R, 0:512], w[2][P:D, 0:512])
            load(wvR[R:P, 0:512], w[2][P:D, 512:1024])
            load(wvR[0:R, 512:1024], w[2][P:D, 1024:1536])
            for m, t in enumerate((wq, wk)):
                load_blocks(t[:, :], w[m][0:P, :])
                load_blocks(wqkR[R * m:R * m + R, :], w[m][P:D, :])
            load(wp[:, :, :], W_proj.rearrange("(c r) n -> r c n", r=D)[0:P])
            for j in range(2):
                load(wpR[R * j:R * j + R, :, :], W_proj.rearrange("(p j r) n -> j r p n", j=2, r=D)[j, P:D])
            qk_b = b_qkv[0:2 * HEADS * D].rearrange("(a j n) -> a j n", j=2, n=D)
            row(brow[0:HEADS, :], qk_b[:, 0, 0:P])
            row(brow[HEADS:2 * HEADS, 0:R], qk_b[:, 0, P:D])
            row(brow[HEADS:2 * HEADS, R:P], qk_b[:, 1, P:D])
            row(brow[2 * HEADS:3 * HEADS, :], qk_b[:, 1, 0:P])
            row(bv2[:, :], b_qkv[2 * HEADS * D:3 * HEADS * D][None, :].to_broadcast([GT, HEADS * D]))
            row(b1row[:, :], b1.rearrange("e (c p) -> (e c) p", p=P))
            row(wgrow[:, :], Wg)
            for m, w in enumerate((Wq, Wk, Wv, Wo)):
                row(fstage[:, m * 2 * D:m * 2 * D + D], w[0:P, :])
                row(fstage[0:R, m * 2 * D + D:(m + 1) * 2 * D], w[P:D, :])
            for dst, src in ((boB, bo), (bvB, bv), (g1, ln1_g), (be1, ln1_b), (g2, ln2_g),
                             (be2, ln2_b), (bgB, bg), (gsc, gamma)):
                bcast(dst[:, :], src)
            row(b2B[:, :, :], b2[None, :, :].to_broadcast([P, E, D]))
            sp.wait_ge(zeroed, 2)
            for dst, src in ((fqb, bq), (fkb, bk)):
                for s in range(4):
                    sp.dma_start(dst[32 * s:32 * s + HD, :], src.rearrange("(c s d) -> s d c", s=4, d=HD)[s],
                                 allow_slow_non_contiguous=True).then_inc(ld_small, 16)
            sp.dma_start(w2[:, :, :], W2.rearrange("e (c p) n -> p (e c) n", p=P)).then_inc(ld_w2, 16)
            sp.sem_inc(stored, 16)
            out_v = out.rearrange("(j s) t d -> j t s d", s=2)

            def move_values(at):
                for s in range(2):
                    sp.wait_ge(drained, drain_no(at, VU[3 * s + 2]) + 1)
                    for g in range(HEADS):
                        sp.dma_start(v2[:, HEADS * s + g, :], vp[g * GT:(g + 1) * GT, s, :]).then_inc(v_moved[s], 16)

            def store(j):
                sp.wait_ge(out_ready, j + 1)
                sp.dma_start(out_v[ds(j, 1)].rearrange("a t s d -> t (a s) d"), res[:, :, :]).then_inc(stored, 16)

            move_values(("first", 0))
            move_values(("peel", 0))
            with sp.Fori(1, PAIRS - 1, 1) as i:
                move_values(("loop", i - 1))
                store(i - 1)
            store(PAIRS - 2)
            store(PAIRS - 1)
            sp.wait_ge(stored, 16 * (PAIRS + 1))

        @block.gpsimd
        def _(pool):
            pool.memset(fqb[:, :], 0.0).then_inc(zeroed, 1)
            pool.memset(fkb[:, :], 0.0).then_inc(zeroed, 1)
            for t in (fqH, fqL, fqS, fkH, fkL, fkS):
                pool.memset(t[:, :].bitcast(f32), 0.0).then_inc(zeroed, 1)
            pool.memset(ones[:, :], 1.0).then_inc(zeroed, 1)
            pool.memset(ident[:, :], 0.0).then_inc(zeroed, 1)
            pool.wait_ge(zeroed, 10)
            pool.affine_select(out=ident[:, :], in_=ident[:, :], compare_op=ALU.not_equal, fill=1.0, base=0,
                               pattern=[[-1, P]], channel_multiplier=1).then_inc(const_ready, 1)
            pool.affine_select(out=upper[:, :], in_=ones[0:S, 0:S], compare_op=ALU.is_ge, fill=0.0, base=0,
                               pattern=[[1, S]], channel_multiplier=-1).then_inc(const_ready, 1)
            pool.iota(iota[:, :], pattern=[[1, T]], base=0, channel_multiplier=0,
                      allow_small_or_imprecise_dtypes=True).then_inc(const_ready, 1)
            pool.memset(earlier[:, :, :], 0.0).then_inc(const_ready, 1)
            pool.memset(mhalf[:, :], -0.5).then_inc(const_ready, 1)
            pool.memset(half[:, :], 0.5).then_inc(const_ready, 1)

            def gathers(i):
                pool.wait_ge(idx_ready, i + 1)
                pool.sem_inc(gather_go, 1)
                for s in range(2):
                    pool.indirect_dma_start(out=rows[0:HALF, s, :], out_offset=None, in_=word_emb,
                                            in_offset=bass.IndirectOffsetOnAxis(ap=idxw[:, s:s + 1], axis=0))\
                        .then_inc(got_words, 16)
                pool.indirect_dma_start(out=entg[:, :], out_offset=None, in_=ent_emb,
                                        in_offset=bass.IndirectOffsetOnAxis(ap=idxk[:, 0:1], axis=0))\
                    .then_inc(got_ents, 16)

            def inverse_root(kind, i):
                pool.wait_ge(var_ready[kind], i + 1)
                pool.tensor_tensor(out=rstd[:, :], in0=ve[:, :], in1=mhalf[:, :], op=ALU.pow)\
                    .then_inc(rstd_ready[kind], 1)

            def value_bias(i):
                for s in range(2):
                    pool.wait_ge(v_moved[s], 16 * HEADS * (i + 1))
                    v = v2[:, HEADS * s:HEADS * (s + 1), :]
                    pool.tensor_tensor(out=v, in0=v, in1=bv2[:, None, :].to_broadcast([P, HEADS, D]), op=ALU.add)\
                        .then_inc(v_ready, 1)

            def roots(i):
                for k in range(4):
                    pool.wait_ge(f_var, 4 * i + k + 1)
                    pool.tensor_tensor(out=fsd[:, :], in0=fvar[:, :], in1=half[:, :], op=ALU.pow).then_inc(f_sd, 1)

            gathers(0)
            inverse_root("t", 0)
            inverse_root("a", 0)
            pool.wait_ge(ld_small, 16 * SMALL)
            gathers(1)
            value_bias(0)
            inverse_root("b", 0)
            inverse_root("t", 1)
            inverse_root("a", 1)
            roots(0)
            value_bias(1)
            with pool.Fori(1, PAIRS - 1, 1) as i:
                inverse_root("x", i - 1)
                gathers(i + 1)
                inverse_root("b", i)
                inverse_root("t", i + 1)
                inverse_root("a", i + 1)
                roots(i)
                inverse_root("o", i - 1)
                value_bias(i + 1)
            inverse_root("x", PAIRS - 2)
            inverse_root("b", PAIRS - 1)
            roots(PAIRS - 1)
            inverse_root("o", PAIRS - 2)
            inverse_root("x", PAIRS - 1)
            inverse_root("o", PAIRS - 1)

        @block.scalar
        def _(act):
            def drain(at, name, *ops):
                act.wait_ge(filled, drain_no(at, name) + 1)
                for dst, src in ops[:-1]:
                    act.activation(dst, src, ACT.Copy)
                act.activation(*ops[-1], ACT.Copy).then_inc(drained, 1)

            W = ("ids", 0)
            drain(W, "ids", (idT[:, :, :], place(W, "ids")[0:S, 0:2 * B].rearrange("p (a b) -> p a b", a=2)))
            drain(W, "prefix", (pref[:, :, :], place(W, "prefix")[0:S, 0:2 * B].rearrange("p (a b) -> p a b", a=2)))
            drain(W, "ke_w", (kewT[:, :], place(W, "ke_w")[0:D_ENT, 0:D]))

            def entities(at, i):
                drain(at, "ent", (entT[:, :], place(at, "ent")[0:D_ENT, 0:P]))

            def projected(at, i):
                act.wait_ge(filled, drain_no(at, "proj") + 1)
                u = place(at, "proj")
                act.activation(rows[HALF:P, 0, :], u[HALF:P, 0:D], ACT.Copy, scale=emb[HALF:P, 0, D + 1:D + 2])
                act.activation(rows[HALF:P, 1, :], u[HALF:P, D:2 * D], ACT.Copy, scale=emb[HALF:P, 1, D + 1:D + 2])\
                   .then_inc(drained, 1)

            def whole(at, name, dst):
                drain(at, name, (dst, place(at, name)[:, :]))

            def index(at):
                drain(at, "index", (emb[:, :, :].rearrange("p s n -> p (s n)"), place(at, "index")[:, 0:2 * XW]))

            def projected_rows(at, m, lo, hi):
                t = (qt, kt)[m]
                main = t[:, 0:NM].rearrange("p (n c) -> p c n", c=HEADS)
                rest = t[:, NM:NM + NR].rearrange("p (n c) -> p c n", c=HEADS)
                for n in range(lo, hi):
                    name = (QU, KU)[m][n]
                    u = place(at, name)
                    act.wait_ge(filled, drain_no(at, name) + 1)
                    for k in range(2):
                        p, x = divmod(2 * n + k, 3)
                        col = slice(x * HEADS + m * HP + p, x * HEADS + m * HP + p + 1)
                        if x != 1:
                            ins = act.activation(main[:, 2 * p + x // 2, :], u[:, k * NT:(k + 1) * NT], ACT.Identity,
                                                 bias=qkbias[:, col])
                            continue
                        for j in range(2):
                            r = slice(R * j, R * j + R)
                            for s in range(2):
                                ins = act.activation(rest[R * s:R * s + R, 2 * p + j, :],
                                                     u[r, k * NT + s * T:k * NT + (s + 1) * T], ACT.Identity,
                                                     bias=qkbias[r, col])
                    ins.then_inc(drained, 1)

            def values(at, n):
                whole(at, VU[n], vp[:, n // 3, n % 3 * 512:(n % 3 + 1) * 512])

            def outputs(at, s):
                for u in (2 * s, 2 * s + 1):
                    drain(at, f"om{u}", (oT[:, :, u * NT // 4:(u + 1) * NT // 4],
                                         place(at, f"om{u}")[:, :].rearrange("p (n c) -> p c n", c=HEADS)))
                drain(at, f"or{s}", (oR[:, :, s * T:(s + 1) * T],
                                     place(at, f"or{s}")[:, :].rearrange("p (n c) -> p c n", c=HP)))

            def attn_exp(i, u):
                act.wait_ge(a_max, 4 * i + u + 1)
                for k in range(4):
                    act.activation(prob[:, u, k, :], unit_of(u)[:, k, :], ACT.Exp, bias=nmax[:, u, k:k + 1],
                                   accum_out=asum[:, u, k:k + 1]).then_inc(a_exp, 1)

            def ffn_exp(i, u):
                k, s = u // 2, u % 2
                act.wait_ge(f_scale, 4 * i + k + 1)
                for c in range(FCH):
                    n = FCH * s + c
                    act.activation(prob[:, u % 4, c, :], unit_of(u)[:, c, :], ACT.Exp, bias=fnb[:, k, n:n + 1],
                                   scale=fsc[:, k, n:n + 1], accum_out=fsum[:, s, 4 * c + k:4 * c + k + 1])\
                       .then_inc(f_exp, 1)

            def expert_up(at, n):
                u = place(at, UP[n])
                act.wait_ge(filled, drain_no(at, UP[n]) + 1)
                for k in range(2):
                    c = 2 * n + k
                    ins = act.activation(hid[:, c // KCH % 2, c % KCH, :], u[:, k * NT:(k + 1) * NT], ACT.Relu,
                                         bias=b1c[:, c:c + 1])
                ins.then_inc(drained, 1)

            def ffn_projections(at):
                for c in range(FCH):
                    u = place(at, f"qk{c}")
                    act.wait_ge(filled, drain_no(at, f"qk{c}") + 1)
                    act.activation(fqT[:, c, :], u[:, 0:NT], ACT.Identity, bias=fqb[:, c:c + 1], scale=qscale[:, 0:1])
                    act.activation(fkT[:, c, :], u[:, NT:2 * NT], ACT.Identity, bias=fkb[:, c:c + 1])\
                       .then_inc(drained, 1)
                drain(at, "fval", (fval[:, :, :].rearrange("p s n -> p (s n)"), place(at, "fval")[:, 0:2 * D]))

            def ffn_out_turned(at):
                u = place(at, "attnT")
                drain(at, "attnT", (foT[:, 0, :], u[:, 0:NT]), (foT[0:R, 1, :], u[0:R, NT:2 * NT]))

            def ffn_out(at):
                drain(at, "wo", (fwo[:, :, :].rearrange("p s n -> p (s n)"), place(at, "wo")[:, 0:2 * D]))

            def gate_exps(j):
                act.wait_ge(gate_shift, j + 1)
                act.activation(gx[:, :, :], gs[:, :, :], ACT.Exp).then_inc(gate_exp, 1)

            at = ("first", 0)
            index(at)
            entities(at, 0)
            projected(at, 0)
            act.wait_ge(ld_w1, 32)
            act.activation(w1H[:, :], w1A, ACT.Copy).then_inc(w1_hi, 1)
            act.activation(w1S[0:R, :], w1B, ACT.Copy).then_inc(w1_hi, 1)
            u, nb = place(at, "small"), 2 * QCH
            drain(at, "small", (b1c[:, :], u[:, 0:nb]), (qkbias[:, :], u[:, nb:2 * nb]),
                  (wgT[:, 0:E], u[:, 2 * nb:2 * nb + E]), (wgT[0:R, E:2 * E], u[0:R, 2 * nb + E:2 * nb + 2 * E]))
            for m, name in enumerate(("fq", "fk", "fv", "fo")):
                u = place(at, name)
                drain(at, name, (fqk[m][:, 0:D], u[:, 0:D]), (fqk[m][0:R, D:2 * D], u[0:R, D:2 * D]))
            whole(at, "aT", aT[:, :])
            act.wait_ge(w1_split, 1)
            for n in range(6):
                values(at, n)
            projected_rows(at, 0, 0, 6)

            def step(at, i, full, ahead=True):
                projected_rows(at, 1, 0, 3)
                if full:
                    ffn_out_turned(at)
                else:
                    index(at)
                projected_rows(at, 1, 3, 6)
                if full:
                    ffn_out(at)
                if full and ahead:
                    index(at)
                for u in range(4):
                    attn_exp(i, u)
                outputs(at, 0)
                outputs(at, 1)
                if full:
                    whole(at, "xT", xT[:, :])
                if ahead:
                    entities(at, i + 1)
                if full:
                    for n in range(3):
                        expert_up(at, n)
                    if ahead:
                        projected(at, i + 1)
                    gate_exps(i - 1)
                    for n in range(3, 6):
                        expert_up(at, n)
                whole(at, "bT", bT[:, :])
                if full:
                    for n in range(6, 12):
                        expert_up(at, n)
                    if ahead:
                        whole(at, "aT", aT[:, :])
                    ffn_projections(at)
                else:
                    projected(at, i + 1)
                    ffn_projections(at)
                    whole(at, "aT", aT[:, :])
                for u in range(FU):
                    ffn_exp(i, u)
                    if ahead and u in (1, 3, 5):
                        for n in ((0, 1), (2, 3, 4), (5,))[u // 2]:
                            values(at, n)
                    if ahead and u == 5:
                        projected_rows(at, 0, 0, 3)
                if ahead:
                    projected_rows(at, 0, 3, 6)

            step(("peel", 0), 0, False)
            with act.Fori(1, PAIRS - 1, 1) as i:
                step(("loop", i - 1), i, True)
            step(("final", 0), PAIRS - 1, True, ahead=False)
            at = ("last", 0)
            ffn_out_turned(at)
            ffn_out(at)
            whole(at, "xT", xT[:, :])
            for n in range(12):
                expert_up(at, n)
                if n == 2:
                    gate_exps(PAIRS - 1)

        @block.vector
        def _(dve):
            one = Steps(dve, pro_step, 0, 34)

            def link(ins):
                one.did(ins)
                one.wait()

            dve.wait_ge(ld_ids, 32)
            dve.tensor_copy(ids_f[:, :, :], ids_i[:, :, :]).then_inc(ids_ready, 1)
            dve.wait_ge(drained, drain_no(("ids", 0), "ids") + 1)
            link(dve.tensor_scalar(kmask[:, 0, :], idT[:, 0, :], 0.0, None, ALU.is_gt))
            link(dve.scalar_tensor_tensor(out=kmask[:, 0, :], in0=idT[:, 0, :], scalar=float(VOCAB),
                                          in1=kmask[:, 0, :], op0=ALU.is_lt, op1=ALU.mult))
            dve.tensor_scalar(kmask[:, 1, :], idT[:, 0, :], float(VOCAB), None, ALU.is_ge).then_inc(mask_ready, 1)
            dve.wait_ge(mask_ready, 1)
            link(dve.memset(val[:, :], 0.0))
            link(dve.memset(slot[:, :], -1.0))
            link(dve.memset(ttv[:, :], 0.0))
            link(dve.memset(embR[:, :, :], 1.0))
            link(dve.scalar_tensor_tensor(out=val[:, 0:B], in0=kmask[:, 1, :], scalar=-float(VOCAB), in1=idT[:, 0, :],
                                          op0=ALU.mult, op1=ALU.add))
            link(dve.tensor_copy(ttv[:, 0:B], idT[:, 1, :]))
            dve.memset(sgn[0:HALF, :], -1.0)
            dve.memset(sgn[HALF:P, :], 1.0)
            dve.memset(off[0:HALF, :], 1.0)
            link(dve.memset(off[HALF:P, :], 0.0))
            dve.wait_ge(drained, drain_no(("ids", 0), "prefix") + 1)
            link(dve.scalar_tensor_tensor(out=kmask[:, :, :], in0=pref[:, :, :], scalar=float(HALF) + 0.5,
                                          in1=kmask[:, :, :], op0=ALU.is_lt, op1=ALU.mult))
            link(dve.tensor_scalar(pref[:, 1, :], pref[:, 1, :], float(HALF), None, ALU.add))
            link(dve.tensor_tensor(out=pref[:, :, :], in0=pref[:, :, :], in1=kmask[:, :, :], op=ALU.mult))
            link(dve.tensor_tensor(out=slot[:, 0:B], in0=pref[:, 0, :], in1=pref[:, 1, :], op=ALU.add))
            link(dve.tensor_scalar(slot[:, 0:B], slot[:, 0:B], -1.0, None, ALU.add))
            dve.wait_ge(ld_tok, 16 * TOK)
            dve.wait_ge(zeroed, 10)
            dve.wait_ge(const_ready, 6)
            for e in range(1, E):
                link(dve.memset(earlier[:, e, 0:e], 1.0))
            link(dve.tensor_tensor(out=ttd[:, :], in0=ttd[:, :], in1=tt0[:, :], op=ALU.subtract))
            link(dve.tensor_tensor(out=post[:, :], in0=post[:, :], in1=tt0[:, :], op=ALU.add))
            link(dve.tensor_tensor(out=slotC[0:HALF, :], in0=slotC[0:HALF, :], in1=rows[0:HALF, 0, :], op=ALU.add))

            def build_onehot(i):
                k = Steps(dve, index_step, i, 6)
                for s in range(2):
                    col = ds(2 * i + s, 1)
                    k.did(dve.tensor_scalar(onehot[:, s, :], iota[:, :], slot[:, col], None, ALU.is_equal))
                    k.did(dve.scalar_tensor_tensor(out=embR[:, s, 0:D], in0=ttd[:, :], scalar=ttv[:, col],
                                                   in1=post[:, :], op0=ALU.mult, op1=ALU.add))
                    k.did(dve.tensor_copy(embR[:, s, D:D + 1], val[:, col]))
                k.end()
                k.wait()
                dve.sem_inc(onehot_ready, 1)

            def build_index(at, i):
                dve.wait_ge(drained, drain_no(at, "index") + 1)
                dve.tensor_copy(idxw[:, :], emb[0:HALF, :, D:D + 1].rearrange("p s o -> p (s o)"))
                for s in range(2):
                    ins = dve.tensor_scalar(idxk[s * HALF:(s + 1) * HALF, :], emb[HALF:P, s, D:D + 1],
                                            float(N_ENT - 1), None, ALU.min)
                ins.then_inc(idx_ready, 1)

            def normalise(k, kind, i, src, dst, eps):
                for s in range(2):
                    k.did(dve.bn_stats(st[:, s, :], src[:, s, :]))
                k.wait()
                dve.sem_inc(stats_seen, 1)
                for s in range(2):
                    k.did(dve.bn_aggr(mv[:, s, :], st[:, s, :]))
                k.wait()
                dve.tensor_scalar(ve[:, :], mv[:, :, 1:2].rearrange("p s o -> p (s o)"), eps, None, ALU.add)\
                   .then_inc(var_ready[kind], 1)
                dve.wait_ge(rstd_ready[kind], i + 1)
                for s in range(2):
                    k.did(dve.tensor_scalar(dst[:, s, 0:D], src[:, s, :], mv[:, s, 0:1], rstd[:, s:s + 1],
                                            ALU.subtract, ALU.mult))
                k.wait()

            def over(v):
                return v[:, None, :].to_broadcast([P, 2, D])

            def affine(k, t, g, b):
                k.did(dve.tensor_tensor(out=t, in0=t, in1=over(g), op=ALU.mult))
                k.wait()
                k.did(dve.tensor_tensor(out=t, in0=t, in1=over(b), op=ALU.add))
                k.wait()

            def twice(t, ready):
                dve.tensor_copy(t[:, :, D:2 * P], t[:, :, P:D]).then_inc(ready, 1)

            def split(at, name, src, H, L, ready, n):
                dve.wait_ge(drained, drain_no(at, name) + 1)
                dve.tensor_copy(H[:, :], src[:, :]).then_inc(ready, 1)
                dve.wait_ge(ready, 2 * n + 1)
                dve.tensor_tensor(out=L[:, :], in0=src[:, :], in1=H[:, :].bitcast(f32), op=ALU.subtract).then_inc(ready, 1)

            def embed(k, at, i):
                dve.wait_ge(drained, drain_no(at, "proj") + 1)
                dve.wait_ge(got_words, 32 * (i + 1))
                k.did(dve.tensor_tensor(out=rows[:, :, :], in0=rows[:, :, :], in1=emb[:, :, 0:D], op=ALU.add))
                k.did(dve.tensor_scalar(coef[:, :], emb[:, :, D + 1:D + 2].rearrange("p s o -> p (s o)"), sgn[:, 0:1],
                                        off[:, 0:1], ALU.mult, ALU.add))
                k.wait()
                for s in range(2):
                    k.did(dve.scalar_tensor_tensor(out=rows[:, s, :], in0=slotC[:, :], scalar=coef[:, s:s + 1],
                                                   in1=rows[:, s, :], op0=ALU.mult, op1=ALU.add))
                k.wait()
                normalise(k, "t", i, rows, h0, EPS_TOK)
                affine(k, h0[:, :, :], gam, bet)

            def attn_input(k, i):
                normalise(k, "a", i, h0, aD, EPS)
                twice(aD, aD_ready)
                k.did(dve.tensor_tensor(out=h0[:, :, :], in0=h0[:, :, :], in1=over(obias), op=ALU.add))
                k.wait()
                k.did(dve.tensor_copy(coef[:, 0:1], sgn[:, 0:1]))
                k.end()

            def attn_max(i, u):
                dve.wait_ge(a_scores, 4 * i + u + 1)
                dve.tensor_reduce(nmax[:, u, :], unit_of(u)[:, :, :], AX.X, ALU.max, negate=True).then_inc(a_max, 1)

            def attn_norm(k, i, u):
                dve.wait_ge(a_exp, 16 * i + 4 * u + 4)
                k.did(dve.reciprocal(arec[:, u, :], asum[:, u, :]))
                k.wait()
                for n in range(4):
                    ins = dve.tensor_scalar(prob[:, u, n, :], prob[:, u, n, :], arec[:, u, n:n + 1], D ** -0.5,
                                            ALU.mult, ALU.mult)
                ins.then_inc(a_prob, 1)

            def attn_turn(i, u):
                dve.wait_ge(a_turned, 4 * i + u + 1)
                dve.tensor_copy(probT[:, u % 2, :, :], unit_of(u)[:, :, :]).then_inc(a_probT, 1)

            def attn_out(k, at, i):
                dve.wait_ge(acc_filled, sum_no(at, "attn") + 1)
                dve.tensor_tensor(out=h1[:, :, :].rearrange("p s n -> p (s n)"), in0=acc[:, 0:2 * D],
                                  in1=h0[:, :, :].rearrange("p s n -> p (s n)"), op=ALU.add).then_inc(acc_drained, 1)
                dve.wait_ge(acc_drained, sum_no(at, "attn") + 1)
                normalise(k, "b", i, h1, bD, EPS)
                twice(bD, bD_ready)

            def ffn_tail(at, j):
                k = Steps(dve, ftail_step, j, 10)
                k.did(dve.tensor_tensor(out=pre[:, :, :], in0=bD[:, :, 0:D], in1=over(boB), op=ALU.add))
                k.wait()
                dve.wait_ge(drained, drain_no(at, "wo") + 1)
                k.did(dve.tensor_tensor(out=pre[:, :, :], in0=pre[:, :, :], in1=fwo[:, :, :], op=ALU.add))
                k.wait()
                normalise(k, "x", j, pre, xD, EPS)
                affine(k, xD[:, :, 0:D], g1, be1)
                twice(xD, xD_ready)
                k.end()

            def gate(k, j):
                dve.wait_ge(gate_ready, j + 1)
                k.did(dve.tensor_tensor(out=gl[:, :, :], in0=acc[:, 2 * D:2 * D + 2 * E].rearrange("p (s e) -> p s e", s=2),
                                        in1=bgB[:, None, :].to_broadcast([P, 2, E]), op=ALU.add))
                k.wait()
                k.did(dve.tensor_reduce(gm[:, :], gl[:, :, :], AX.X, ALU.max))
                k.wait()
                dve.tensor_tensor(out=gs[:, :, :], in0=gl[:, :, :], in1=gm[:, :, None].to_broadcast([P, 2, E]),
                                  op=ALU.subtract).then_inc(gate_shift, 1)
                dve.wait_ge(gate_exp, j + 1)
                k.did(dve.tensor_reduce(gsum[:, :], gx[:, :, :], AX.X, ALU.add))
                k.wait()
                k.did(dve.reciprocal(grec[:, :], gsum[:, :]))
                k.wait()
                k.did(dve.tensor_tensor(out=gp[:, :, :], in0=gx[:, :, :], in1=grec[:, :, None].to_broadcast([P, 2, E]),
                                        op=ALU.mult))
                k.wait()
                other = gp[:, :, None, :].to_broadcast([P, 2, E, E])
                own = gp[:, :, :, None].to_broadcast([P, 2, E, E])
                k.did(dve.tensor_tensor(out=ggt[:, :, :, :], in0=other, in1=own, op=ALU.is_gt))
                k.did(dve.tensor_tensor(out=gge[:, :, :, :], in0=other, in1=own, op=ALU.is_equal))
                k.wait()
                k.did(dve.tensor_tensor(out=gge[:, :, :, :], in0=gge[:, :, :, :],
                                        in1=earlier[:, None, :, :].to_broadcast([P, 2, E, E]), op=ALU.mult))
                k.wait()
                k.did(dve.tensor_tensor(out=ggt[:, :, :, :], in0=ggt[:, :, :, :], in1=gge[:, :, :, :], op=ALU.add))
                k.wait()
                k.did(dve.tensor_reduce(grk[:, :, :], ggt[:, :, :, :], AX.X, ALU.add))
                k.wait()
                k.did(dve.scalar_tensor_tensor(out=comb[:, :, :], in0=grk[:, :, :], scalar=1.5, in1=gp[:, :, :],
                                               op0=ALU.is_lt, op1=ALU.mult))
                k.wait()
                for s in range(2):
                    for e in range(E):
                        src = xD[:, s, 0:D] if e == 0 else ff[:, s, :]
                        k.did(dve.scalar_tensor_tensor(out=ff[:, s, :], in0=b2B[:, e, :], scalar=comb[:, s, e:e + 1],
                                                       in1=src, op0=ALU.mult, op1=ALU.add))
                        k.wait()

            def expert_out(k, at, e):
                dve.wait_ge(acc_filled, sum_no(at, f"y{e}") + 1)
                k.did(dve.scalar_tensor_tensor(out=ff[:, 0, :], in0=acc[:, 0:D], scalar=comb[:, 0, e:e + 1],
                                               in1=ff[:, 0, :], op0=ALU.mult, op1=ALU.add))
                dve.scalar_tensor_tensor(out=ff[:, 1, :], in0=acc[:, D:2 * D], scalar=comb[:, 1, e:e + 1],
                                         in1=ff[:, 1, :], op0=ALU.mult, op1=ALU.add).then_inc(acc_drained, 1)
                dve.wait_ge(acc_drained, sum_no(at, f"y{e}") + 1)

            def moe_end(k, j):
                dve.wait_ge(stored, 16 * j + 16)
                normalise(k, "o", j, ff, res, EPS)
                affine(k, res[:, :, :], g2, be2)
                dve.tensor_tensor(out=res[:, :, :], in0=res[:, :, :], in1=h1keep[:, :, :], op=ALU.add).then_inc(out_ready, 1)

            def ffn_values(at, i):
                dve.wait_ge(drained, drain_no(at, "fval") + 1)
                dve.tensor_tensor(out=fval[:, :, :], in0=fval[:, :, :], in1=over(bvB), op=ALU.add).then_inc(fval_ready, 1)

            def ffn_scales(k, i, strip):
                for s in range(2):
                    u = 2 * strip + s
                    dve.wait_ge(f_scores, FU * i + u + 1)
                    for c in range(FCH):
                        k.did(dve.bn_stats(fst[:, FCH * s + c, :], unit_of(u)[:, c, :]))
                    k.did(dve.tensor_reduce(fmax[:, FCH * s:FCH * (s + 1)], unit_of(u)[:, 0:FCH, :], AX.X, ALU.max))
                k.wait()

                def stat(n):
                    return fst[:, :, n:n + 1].rearrange("p n o -> p (n o)")

                k.did(dve.tensor_tensor(out=fd[:, :], in0=stat(1), in1=stat(4), op=ALU.subtract))
                k.did(dve.tensor_tensor(out=fm2[:, :], in0=stat(2), in1=stat(5), op=ALU.add))
                k.wait()
                k.did(dve.scalar_tensor_tensor(out=fw[:, :], in0=fd[:, :], scalar=T / 4.0, in1=fd[:, :],
                                               op0=ALU.mult, op1=ALU.mult))
                k.wait()
                dve.tensor_tensor(out=fvar[:, :], in0=fw[:, :], in1=fm2[:, :], op=ALU.add).then_inc(f_var, 1)
                dve.wait_ge(f_sd, 4 * i + strip + 1)
                k.did(dve.tensor_scalar(fden[:, strip, :], fsd[:, :], (T - 1.0) ** -0.5, EPS, ALU.mult, ALU.add))
                k.wait()
                k.did(dve.reciprocal(finv[:, strip, :], fden[:, strip, :]))
                k.wait()
                k.did(dve.tensor_scalar(fsc[:, strip, :], finv[:, strip, :], gabs[:, 0:1], None, ALU.mult))
                k.wait()
                dve.scalar_tensor_tensor(out=fnb[:, strip, :], in0=fmax[:, :], scalar=-1.0, in1=fsc[:, strip, :],
                                         op0=ALU.mult, op1=ALU.mult).then_inc(f_scale, 1)
                dve.wait_ge(f_scale, 4 * i + strip + 1)

            def ffn_turn(i, u):
                dve.wait_ge(f_turned, FU * i + u + 1)
                dve.tensor_copy(probT[:, u % 2, 0:FCH, :], unit_of(u)[:, 0:FCH, :]).then_inc(f_probT, 1)

            def ffn_heads(k, at, i):
                dve.wait_ge(f_exp, FU * FCH * (i + 1))
                k.did(dve.reciprocal(frec[:, :, :], fsum[:, :, :]))
                k.wait()
                dve.wait_ge(acc_filled, sum_no(at, "ffn") + 1)
                dve.tensor_tensor(out=fo[:, :, :].rearrange("p s (h w) -> p (s h) w", w=HD),
                                  in0=acc[:, 0:2 * D].rearrange("p (g w) -> p g w", w=HD),
                                  in1=frec[:, :, :].rearrange("p s h -> p (s h)")[:, :, None].to_broadcast([P, 2 * FHEADS, HD]),
                                  op=ALU.mult).then_inc(acc_drained, 1)

            at = ("first", 0)
            build_onehot(0)
            build_index(at, 0)
            k = Steps(dve, tok_step, 0, 20)
            embed(k, at, 0)
            attn_input(k, 0)
            dve.wait_ge(w1_hi, 2)
            link(dve.tensor_tensor(out=w1L[:, :], in0=w1A, in1=w1H[:, :].bitcast(f32), op=ALU.subtract))
            dve.tensor_tensor(out=w1S[R:P, :], in0=w1B, in1=w1S[0:R, :].bitcast(f32), op=ALU.subtract).then_inc(w1_split, 1)
            dve.wait_ge(ld_small, 16 * SMALL)
            link(dve.tensor_scalar(qscale[:, :], gsc[:, :], 0.0, None, ALU.is_ge))
            link(dve.tensor_scalar(qscale[:, :], qscale[:, :], 2.0, -1.0, ALU.mult, ALU.add))
            link(dve.tensor_tensor(out=gabs[:, :], in0=gsc[:, :], in1=qscale[:, :], op=ALU.mult))
            link(dve.tensor_scalar(qscale[:, :], qscale[:, :], HD ** -0.5, None, ALU.mult))
            link(dve.tensor_scalar(fqb[:, :], fqb[:, :], qscale[:, 0:1], None, ALU.mult))
            dve.wait_ge(drained, drain_no(("first", 0), "fk") + 1)
            for m, (H, L, St) in enumerate(((fqH, fqL, fqS), (fkH, fkL, fkS))):
                def heads(t, rows_):
                    return t[rows_, :].rearrange("p (h w) -> p h w", w=32)[:, :, 0:HD]
                main = fqk[m][:, 0:D].rearrange("p (h w) -> p h w", w=HD)
                rest = fqk[m][0:R, D:2 * D].rearrange("p (h w) -> p h w", w=HD)
                a, r, q = slice(0, P), slice(0, R), slice(R, P)
                link(dve.tensor_copy(heads(H, a), main))
                link(dve.tensor_tensor(out=heads(L, a), in0=main, in1=heads(H, a).bitcast(f32), op=ALU.subtract))
                link(dve.tensor_copy(heads(St, r), rest))
                link(dve.tensor_tensor(out=heads(St, q), in0=rest, in1=heads(St, r).bitcast(f32), op=ALU.subtract))

            def step(at, i, full, ahead=True):
                kn = Steps(dve, tok_step, i + 1, 20) if ahead else None
                ka = Steps(dve, attn_step, i, 11)
                kf = Steps(dve, ffn_step, i, 57)
                km = Steps(dve, moe_step, i - 1, 31) if full else None
                if ahead:
                    build_onehot(i + 1)
                if not full:
                    build_index(at, i + 1)
                if full:
                    ffn_tail(at, i - 1)
                    if ahead:
                        build_index(at, i + 1)
                attn_max(i, 0)
                attn_max(i, 1)
                attn_norm(ka, i, 0)
                attn_max(i, 2)
                attn_norm(ka, i, 1)
                attn_max(i, 3)
                attn_turn(i, 0)
                attn_norm(ka, i, 2)
                attn_turn(i, 1)
                attn_norm(ka, i, 3)
                attn_turn(i, 2)
                attn_turn(i, 3)
                if full:
                    split(at, "xT", xT, xH, xL, x_split, i - 1)
                attn_out(ka, at, i)
                if full:
                    gate(km, i - 1)
                    if ahead:
                        embed(kn, at, i + 1)
                    expert_out(km, at, 0)
                    if ahead:
                        attn_input(kn, i + 1)
                    expert_out(km, at, 1)
                    dve.wait_ge(drained, drain_no(at, UP[-1]) + 1)
                split(at, "bT", bT, bH, bL, b_split, i)
                if full:
                    expert_out(km, at, 2)
                else:
                    embed(kn, at, i + 1)
                    attn_input(kn, i + 1)
                ffn_scales(kf, i, 0)
                ffn_scales(kf, i, 1)
                ffn_values(at, i)
                if full:
                    expert_out(km, at, 3)
                ffn_turn(i, 0)
                ffn_turn(i, 1)
                ffn_scales(kf, i, 2)
                ffn_turn(i, 2)
                ffn_turn(i, 3)
                ffn_scales(kf, i, 3)
                for u in range(4, FU):
                    ffn_turn(i, u)
                ffn_heads(kf, at, i)
                dve.wait_ge(acc_drained, sum_no(at, "ffn") + 1)
                dve.sem_inc(fo_ready, 1)
                if full:
                    moe_end(km, i - 1)
                    km.end()
                    dve.wait_ge(out_ready, i)
                ka.did(dve.tensor_copy(h1keep[:, :, :], h1[:, :, :]))
                ka.wait()
                ka.end()
                kf.end()

            step(("peel", 0), 0, False)
            with dve.Fori(1, PAIRS - 1, 1) as i:
                step(("loop", i - 1), i, True)
            step(("final", 0), PAIRS - 1, True, ahead=False)
            at = ("last", 0)
            j = PAIRS - 1
            km = Steps(dve, moe_step, j, 31)
            ffn_tail(at, j)
            split(at, "xT", xT, xH, xL, x_split, j)
            gate(km, j)
            for e in range(E):
                expert_out(km, at, e)
            moe_end(km, j)
            km.end()
            one.end()

        @block.tensor
        def _(pe):
            def take(at, name):
                n = drain_no(at, name)
                first = DRAINS[at[0]].index(name) == 0
                need = n if first else n - 2
                if not isinstance(need, int) or need > 0:
                    pe.wait_ge(drained, need)
                return place(at, name)

            def take_acc(at, name):
                n = sum_no(at, name)
                if not isinstance(n, int) or n > 0:
                    pe.wait_ge(acc_drained, n)

            def mm(dst, lhsT, rhs, start=True, stop=True):
                return pe.matmul(dst, lhsT, rhs, start=start, stop=stop)

            def split_weights(dst, w, c, t):
                H, L, St = w
                hi, lo = t
                mm(dst, H[:, c], hi[:, 0:NT], stop=False)
                mm(dst, H[:, c], lo[:, 0:NT], start=False, stop=False)
                mm(dst, L[:, c], hi[:, 0:NT], start=False, stop=False)
                mm(dst, St[:, c], hi[:, NT:2 * NT], start=False, stop=False)
                return mm(dst, St[:, c], lo[:, NT:2 * NT], start=False)

            def turn(dst, src, n):
                return pe.transpose(dst, src, ident[0:n, 0:n])

            W = ("ids", 0)
            pe.wait_ge(const_ready, 2)
            pe.wait_ge(ids_ready, 1)
            u = take(W, "ids")
            turn(u[0:S, 0:B], ids_f[:, 0, :], B)
            turn(u[0:S, B:2 * B], ids_f[:, 1, :], B).then_inc(filled, 1)
            pe.wait_ge(mask_ready, 1)
            u = take(W, "prefix")
            mm(u[0:S, 0:2 * B], upper[:, :], kmask[:, :, :].rearrange("p a b -> p (a b)")).then_inc(filled, 1)
            pe.wait_ge(ld_tok, 16 * TOK)
            u = take(W, "ke_w")
            turn(u[0:D_ENT, 0:P], kwA[:, :], P)
            turn(u[0:D_ENT, P:D], kwB[:, :], R).then_inc(filled, 1)
            def turn_square(u, A, Bt):
                turn(u[:, 0:P], A[:, 0:P], P)
                turn(u[:, P:D], Bt[:, 0:P], R)
                turn(u[0:R, D:D + P], A[:, P:D], P)
                return turn(u[0:R, D + P:2 * D], Bt[:, P:D], R)

            def index(at, i):
                pe.wait_ge(onehot_ready, i + 1)
                u = take(at, "index")
                mm(u[:, 0:XW], onehot[:, 0, :], embR[:, 0, :])
                mm(u[:, XW:2 * XW], onehot[:, 1, :], embR[:, 1, :]).then_inc(filled, 1)

            def entities(at, i):
                pe.wait_ge(got_ents, 16 * i + 16)
                turn(take(at, "ent")[0:D_ENT, 0:P], entg[:, :], P).then_inc(filled, 1)

            def project_entities(at, i):
                u = take(at, "proj")
                pe.wait_ge(drained, drain_no(at, "ent") + 1)
                mm(u[HALF:P, 0:D], entT[:, 0:HALF], kewT[:, :])
                mm(u[HALF:P, D:2 * D], entT[:, HALF:P], kewT[:, :]).then_inc(filled, 1)

            def turn_tokens(at, name, t, ready, n):
                pe.wait_ge(ready, n + 1)
                u = take(at, name)
                for c in range(2):
                    for s in range(2):
                        ins = turn(u[:, c * NT + s * T:c * NT + (s + 1) * T], t[:, s, c * P:(c + 1) * P], P)
                ins.then_inc(filled, 1)

            def projected_rows(at, m, lo, hi):
                w, r = (wq, wk)[m], slice(R * m, R * m + R)
                for n in range(lo, hi):
                    u = take(at, (QU, KU)[m][n])
                    for k in range(2):
                        c, dst = slice((2 * n + k) * P, (2 * n + k + 1) * P), u[:, k * NT:(k + 1) * NT]
                        mm(dst, w[:, c], aT[:, 0:NT], stop=False)
                        ins = mm(dst, wqkR[r, c], aT[r, NT:2 * NT], start=False)
                    ins.then_inc(filled, 1)

            def values(at, n):
                s, k = divmod(n, 3)
                r = slice(R * (k % 2), R * (k % 2) + R)
                u = take(at, VU[n])
                mm(u[:, :], aT[:, s * T:(s + 1) * T], wv[:, k * 512:(k + 1) * 512], stop=False)
                mm(u[:, :], aT[r, NT + s * T:NT + (s + 1) * T], wvR[r, k // 2 * 512:(k // 2 + 1) * 512], start=False)\
                    .then_inc(filled, 1)

            def attn_scores(at, i, u):
                s = u // 2
                if u == 0:
                    pe.wait_ge(drained, drain_no(at, KU[-1]) + 1)
                r = slice(R * s, R * s + R)
                for k in range(4):
                    g = 4 * u + k
                    m = slice(g * T, (g + 1) * T)
                    n = slice(NM + (g - s * HEADS) * T, NM + (g - s * HEADS + 1) * T)
                    mm(unit_of(u)[:, k, :], qt[:, m], kt[:, m], stop=False)
                    ins = mm(unit_of(u)[:, k, :], qt[r, n], kt[r, n], start=False)
                ins.then_inc(a_scores, 1)

            def attn_turn(i, u):
                pe.wait_ge(a_prob, 4 * i + u + 1)
                for k in range(4):
                    ins = turn(unit_of(u)[:, k, :], prob[:, u, k, :], P)
                ins.then_inc(a_turned, 1)

            def attn_values(at, i, u):
                s = u // 2
                if u == 0:
                    pe.wait_ge(v_ready, 2 * i + 2)
                pe.wait_ge(a_probT, 4 * i + u + 1)
                main = take(at, f"om{u}")
                for k in range(4):
                    ins = mm(main[:, k * T:(k + 1) * T], v2[:, 4 * u + k, 0:P], probT[:, u % 2, k, :])
                ins.then_inc(filled, 1)
                rest = take(at, f"or{s}") if u % 2 == 0 else place(at, f"or{s}")
                for k in range(4):
                    w = T // 2
                    c = (u % 2 * 4 + k) * w
                    for j in range(2):
                        ins = mm(rest[R * j:R * j + R, c:c + w], v2[:, 4 * u + k, P:D],
                                 probT[:, u % 2, k, :].rearrange("p (n j) -> p j n", j=2)[:, j, :])
                if u % 2:
                    ins.then_inc(filled, 1)

            def attn_out(at, s):
                if s == 0:
                    take_acc(at, "attn")
                pe.wait_ge(drained, drain_no(at, f"or{s}") + 1)
                t, dst = slice(s * T, (s + 1) * T), acc[:, s * D:(s + 1) * D]
                for c in range(HEADS):
                    mm(dst, oT[:, c, t], wp[:, c, :], start=c == 0, stop=False)
                for p in range(HP):
                    ins = mm(dst, oR[:, p, t], wpR[:, p, :], start=False, stop=p == HP - 1)
                if s == 1:
                    ins.then_inc(acc_filled, 1)

            def turn_heads(at, j):
                pe.wait_ge(fo_ready, j + 1)
                u = take(at, "attnT")
                for s in range(2):
                    turn(u[:, s * T:(s + 1) * T], fo[:, s, 0:P], P)
                    ins = turn(u[0:R, NT + s * T:NT + (s + 1) * T], fo[:, s, P:D], P)
                ins.then_inc(filled, 1)

            def out_projection(at):
                u = take(at, "wo")
                pe.wait_ge(drained, drain_no(at, "attnT") + 1)
                for s in range(2):
                    t = slice(s * T, (s + 1) * T)
                    mm(u[:, s * D:(s + 1) * D], foT[:, 0, t], fvo[:, 1, 0:D], stop=False)
                    ins = mm(u[:, s * D:(s + 1) * D], foT[0:R, 1, t], fvo[0:R, 1, D:2 * D], start=False)
                ins.then_inc(filled, 1)

            def gate(at, j):
                take_acc(at, "y0")
                for s in range(2):
                    dst = acc[:, 2 * D + s * E:2 * D + (s + 1) * E]
                    mm(dst, xT[:, s * T:(s + 1) * T], wgT[:, 0:E], stop=False)
                    ins = mm(dst, xT[0:R, NT + s * T:NT + (s + 1) * T], wgT[0:R, E:2 * E], start=False)
                ins.then_inc(gate_ready, 1)

            def expert_up(at, e):
                for n in range(e * KCH // 2, (e + 1) * KCH // 2):
                    u = take(at, UP[n])
                    for k in range(2):
                        c = 2 * n + k
                        ins = split_weights(u[:, k * NT:(k + 1) * NT], (w1H, w1L, w1S), slice(c * P, (c + 1) * P), (xH, xL))
                    ins.then_inc(filled, 1)

            def expert_down(at, j, e):
                take_acc(at, f"y{e}")
                if e == 0:
                    pe.wait_ge(gate_shift, j + 1)
                pe.wait_ge(drained, drain_no(at, UP[(e + 1) * KCH // 2 - 1]) + 1)
                for s in range(2):
                    for k in range(KCH):
                        ins = mm(acc[:, s * D:(s + 1) * D], hid[:, e % 2, k, s * T:(s + 1) * T], w2[:, e * KCH + k, :],
                                 start=k == 0, stop=k == KCH - 1)
                ins.then_inc(acc_filled, 1)

            def ffn_projection(at, c):
                u = take(at, f"qk{c}")
                w = slice(c * P, (c + 1) * P)
                split_weights(u[:, 0:NT], (fqH, fqL, fqS), w, (bH, bL))
                split_weights(u[:, NT:2 * NT], (fkH, fkL, fkS), w, (bH, bL)).then_inc(filled, 1)

            def ffn_value(at):
                u = take(at, "fval")
                for s in range(2):
                    mm(u[:, s * D:(s + 1) * D], bT[:, s * T:(s + 1) * T], fvo[:, 0, 0:D], stop=False)
                    ins = mm(u[:, s * D:(s + 1) * D], bT[0:R, NT + s * T:NT + (s + 1) * T], fvo[0:R, 0, D:2 * D], start=False)
                ins.then_inc(filled, 1)

            def ffn_scores(at, i, u):
                k, s = u // 2, u % 2
                if u == 0:
                    pe.wait_ge(drained, drain_no(at, "qk2") + 1)
                r, t = slice(32 * k, 32 * k + 32), slice(s * T, (s + 1) * T)
                for c in range(FCH):
                    ins = mm(unit_of(u)[:, c, :], fqT[r, c, t], fkT[r, c, t])
                ins.then_inc(f_scores, 1)

            def ffn_turn(i, u):
                pe.wait_ge(f_exp, FU * FCH * i + FCH * (u + 1))
                for c in range(FCH):
                    ins = turn(unit_of(u)[:, c, :], prob[:, u % 4, c, :], P)
                ins.then_inc(f_turned, 1)

            def ffn_values(at, i, u):
                k, s = u // 2, u % 2
                if u == 0:
                    take_acc(at, "ffn")
                    pe.wait_ge(fval_ready, i + 1)
                pe.wait_ge(f_probT, FU * i + u + 1)
                for c in range(FCH):
                    h = 4 * c + k
                    ins = mm(acc[:, s * D + h * HD:s * D + (h + 1) * HD], probT[:, u % 2, c, :], fval[:, s, h * HD:(h + 1) * HD])
                if u == FU - 1:
                    ins.then_inc(acc_filled, 1)

            at = ("first", 0)
            index(at, 0)
            entities(at, 0)
            project_entities(at, 0)
            pe.wait_ge(ld_small, 16 * SMALL)
            u, nb = take(at, "small"), 2 * QCH
            turn(u[:, 0:nb], b1row[:, :], E * KCH)
            turn(u[:, nb:2 * nb], brow[:, :], nb)
            turn(u[:, 2 * nb:2 * nb + E], wgrow[:, 0:P], E)
            turn(u[0:R, 2 * nb + E:2 * nb + 2 * E], wgrow[:, P:D], E).then_inc(filled, 1)
            for m, name in enumerate(("fq", "fk", "fv", "fo")):
                c = m * 2 * D
                turn_square(take(at, name), fstage[:, c:c + D], fstage[0:R, c + D:c + 2 * D]).then_inc(filled, 1)
            turn_tokens(at, "aT", aD, aD_ready, 0)
            pe.wait_ge(ld_attn, 16 * 19)
            pe.wait_ge(w1_split, 1)
            pe.wait_ge(drained, drain_no(at, "aT") + 1)
            for n in range(6):
                values(at, n)
            projected_rows(at, 0, 0, 6)

            def step(at, i, full, ahead=True):
                projected_rows(at, 1, 0, 3)
                if full:
                    turn_heads(at, i - 1)
                else:
                    index(at, i + 1)
                projected_rows(at, 1, 3, 6)
                if full:
                    out_projection(at)
                if full and ahead:
                    index(at, i + 1)
                for u in range(4):
                    attn_scores(at, i, u)
                attn_turn(i, 0)
                attn_turn(i, 1)
                attn_values(at, i, 0)
                attn_turn(i, 2)
                attn_values(at, i, 1)
                attn_turn(i, 3)
                attn_values(at, i, 2)
                attn_values(at, i, 3)
                attn_out(at, 0)
                if full:
                    turn_tokens(at, "xT", xD, xD_ready, i - 1)
                attn_out(at, 1)
                if ahead:
                    entities(at, i + 1)
                if full:
                    pe.wait_ge(x_split, 2 * (i - 1) + 2)
                    expert_up(at, 0)
                    gate(at, i - 1)
                    if ahead:
                        project_entities(at, i + 1)
                    expert_up(at, 1)
                    expert_down(at, i - 1, 0)
                turn_tokens(at, "bT", bD, bD_ready, i)
                if full:
                    expert_up(at, 2)
                    expert_down(at, i - 1, 1)
                    expert_up(at, 3)
                    expert_down(at, i - 1, 2)
                    if ahead:
                        turn_tokens(at, "aT", aD, aD_ready, i + 1)
                else:
                    project_entities(at, i + 1)
                pe.wait_ge(b_split, 2 * i + 2)
                for c in range(FCH):
                    ffn_projection(at, c)
                ffn_value(at)
                for u in range(4):
                    ffn_scores(at, i, u)
                if full:
                    expert_down(at, i - 1, 3)
                if ahead:
                    if not full:
                        turn_tokens(at, "aT", aD, aD_ready, i + 1)
                        pe.wait_ge(drained, drain_no(at, "aT") + 1)
                    values(at, 0)
                    values(at, 1)
                ffn_turn(i, 0)
                ffn_turn(i, 1)
                ffn_values(at, i, 0)
                ffn_scores(at, i, 4)
                ffn_values(at, i, 1)
                ffn_scores(at, i, 5)
                if ahead:
                    values(at, 2)
                ffn_turn(i, 2)
                ffn_turn(i, 3)
                if ahead:
                    values(at, 3)
                ffn_values(at, i, 2)
                ffn_scores(at, i, 6)
                ffn_values(at, i, 3)
                ffn_scores(at, i, 7)
                if ahead:
                    values(at, 4)
                    values(at, 5)
                    projected_rows(at, 0, 0, 1)
                ffn_turn(i, 4)
                ffn_turn(i, 5)
                if ahead:
                    projected_rows(at, 0, 1, 2)
                ffn_values(at, i, 4)
                ffn_values(at, i, 5)
                if ahead:
                    projected_rows(at, 0, 2, 5)
                ffn_turn(i, 6)
                ffn_turn(i, 7)
                if ahead:
                    projected_rows(at, 0, 5, 6)
                ffn_values(at, i, 6)
                ffn_values(at, i, 7)

            pe.wait_ge(ld_w2, 16)
            step(("peel", 0), 0, False)
            with pe.Fori(1, PAIRS - 1, 1) as i:
                step(("loop", i - 1), i, True)
            step(("final", 0), PAIRS - 1, True, ahead=False)
            at = ("last", 0)
            j = PAIRS - 1
            turn_heads(at, j)
            out_projection(at)
            turn_tokens(at, "xT", xD, xD_ready, j)
            pe.wait_ge(x_split, 2 * j + 2)
            gate(at, j)
            expert_up(at, 0)
            expert_up(at, 1)
            expert_down(at, j, 0)
            expert_up(at, 2)
            expert_down(at, j, 1)
            expert_up(at, 3)
            expert_down(at, j, 2)
            expert_down(at, j, 3)


_INS = ["x", "mask_BS_i0_1"] + [f"L0_tok_{n}" for n in (
    "word_emb", "pos_emb", "tt_emb", "entityVec", "ke_w", "ke_b", "w_gamma", "w_beta", "k_gamma", "k_beta")] + [
    f"L0_attn_{n}" for n in ("W_qkv", "b_qkv", "W_proj", "b_proj")] + [
    f"L0_ffn_{n}" for n in ("Wq", "bq", "Wk", "bk", "Wv", "bv", "Wo", "bo", "gamma", "ln1_g", "ln1_b", "ln2_g",
                            "ln2_b", "Wg", "bg", "W1", "b1", "W2", "b2")]


def kernel(**inputs):
    import numpy as _np
    import concourse.bacc as _bacc
    from concourse import mybir as _mybir
    from concourse.bass_utils import run_bass_kernel_spmd as _run

    nc = _bacc.Bacc("TRN2", target_bir_lowering=False, num_devices=1, dynamic_dma_scratch_size=4096)
    arrays, args = {}, []
    for name in _INS:
        a = _np.ascontiguousarray(inputs[name])
        if a.ndim == 0:
            a = a.reshape(1)
        arrays[f"in_{name}_dram"] = a
        args.append(nc.dram_tensor(f"in_{name}_dram", a.shape, _mybir.dt.from_np(a.dtype), kind="ExternalInput").ap())
    args.append(nc.dram_tensor("out_0_dram", (B, T, D), _mybir.dt.float32, kind="ExternalOutput").ap())
    lm_tower_kernel(nc, *args)
    r = _run(nc, [arrays], core_ids=[0])
    return r.results[0]["out_0_dram"]
```

```python
import concourse.bass as bass
from concourse import mybir
from contextlib import ExitStack

B, S = 32, 80
HALF = 64
T = 2 * HALF
VOCAB, N_ENT, D_ENT = 30522, 125000, 100
D = 192
HEADS = 8
FHEADS, HD = 12, 16
E, FF = 4, 768
EPS_TOK, EPS = 1e-12, 1e-5

P = 128
R = D - P
PAIRS = B // 2
NT = 2 * T
HP = HEADS // 2
QCH = 3 * HP
GT = T // HEADS
FCH = FHEADS // 4
FU = 2 * 4
KCH = FF // P
XW = D + 2

UP = [f"up{n}" for n in range(E * KCH // 2)]
ORDER = (0, 1, 2, 3, 5, 4)
QU, KU = ([f"{k}{n}" for n in ORDER] for k in "qk")
VU = [f"v{n}" for n in range(6)]
OU = ["om0", "om1", "or0", "om2", "om3", "or1"]
DRAINS = {
    "ids": ["ids", "prefix", "ke_w"],
    "first": ["index", "ent", "proj", "small", "aT", *QU, *VU, "fq", "fk", "fv", "fo"],
    "peel": [*KU[:3], "index", *KU[3:], *OU, "ent", "bT", "proj", "fval", "qk0", "qk1", "qk2", "aT", *QU, *VU],
    "loop": ["k0", "attnT", "k1", "k2", "wo", *KU[3:], "index", *OU, "xT", "ent", *UP[:3], "proj", *UP[3:6], "bT",
             *UP[6:9], "fval", *UP[9:], "qk0", "qk1", "qk2", "aT", *QU, *VU],
    "final": ["k0", "attnT", "k1", "k2", "wo", *KU[3:], *OU, "xT", *UP[:6], "bT", *UP[6:9], "fval", *UP[9:], "qk0", "qk1", "qk2"],
    "last": ["attnT", "wo", "xT", *UP],
}
SUMS = {
    "peel": ["attn", "ffn"],
    "loop": ["attn", "y0", "y1", "y2", "y3", "ffn"],
    "final": ["attn", "y0", "y1", "y2", "y3", "ffn"],
    "last": ["y0", "y1", "y2", "y3"],
}
TURNS = {"ids": 1, "first": 1, "peel": 1, "loop": PAIRS - 2, "final": 1, "last": 1}


def numbered(orders):
    start, n = {}, 0
    for part, turns in TURNS.items():
        start[part] = n
        n += turns * len(orders.get(part, []))
    return start


DRAIN_START, SUM_START = numbered(DRAINS), numbered(SUMS)
assert len(DRAINS["loop"]) % 3 == 0


def drain_no(at, name):
    part, turn = at
    return turn * len(DRAINS[part]) + DRAIN_START[part] + DRAINS[part].index(name)


def sum_no(at, name):
    part, turn = at
    return turn * len(SUMS[part]) + SUM_START[part] + SUMS[part].index(name)


class Steps:

    def __init__(self, eng, sem, turn, per):
        self.eng, self.sem, self.base, self.per, self.n = eng, sem, turn * per, per, 0

    def did(self, ins):
        self.n += 1
        ins.then_inc(self.sem, 1)

    def wait(self):
        self.eng.wait_ge(self.sem, self.base + self.n)

    def end(self):
        assert self.n == self.per, (self.sem, self.n, self.per)


def lm_tower_kernel(nc, x, mask, word_emb, pos_emb, tt_emb, ent_emb, ke_w, ke_b, w_gamma, w_beta, k_gamma, k_beta,
                    W_qkv, b_qkv, W_proj, b_proj, Wq, bq, Wk, bk, Wv, bv, Wo, bo, gamma, ln1_g, ln1_b,
                    ln2_g, ln2_b, Wg, bg, W1, b1, W2, b2, out):
    f32, f32r, i32 = mybir.dt.float32, mybir.dt.float32r, mybir.dt.int32
    ALU, ACT, AX = mybir.AluOpType, mybir.ActivationFunctionType, mybir.AxisListType
    ds = bass.ds

    with ExitStack() as ctx:
        def sb(name, shape, dt=f32):
            return ctx.enter_context(nc.sbuf_tensor(name, shape, dt))

        def sem(name):
            return ctx.enter_context(nc.semaphore(name))

        wqH, wqL, wqS = (sb(f"wq{k}", [P, HEADS * D], f32r) for k in "HLS")
        wvH, wvL, wvS = (sb(f"wv{k}", [P, HEADS * D], f32r) for k in "HLS")
        wk = sb("wk", [P, HEADS * D])
        wkR = sb("wkR", [P, HEADS * D // 2])
        wp, wpR = sb("wp", [P, HEADS, D]), sb("wpR", [P, HP, D])
        bv2 = sb("bv2", [P, D])
        w1H, w1L, w1S = (sb(f"w1{k}", [P, E * FF], f32r) for k in "HLS")
        w2 = sb("w2", [P, E * KCH, D])
        fqH, fqL, fqS = (sb(f"fq{k}", [P, FCH * P], f32r) for k in "HLS")
        fkH, fkL, fkS = (sb(f"fk{k}", [P, FCH * P], f32r) for k in "HLS")
        fvo = sb("fvo", [P, 2, 2 * D])
        kewT = sb("kewT", [D_ENT, D])
        wgT = sb("wgT", [P, 2 * E])
        b1c = sb("b1c", [P, E * KCH])
        qkbias = sb("qkbias", [P, 2 * QCH])
        fqb, fkb = sb("fqb", [P, FCH]), sb("fkb", [P, FCH])
        qscale, gabs = sb("qscale", [P, 1]), sb("gabs", [P, 1])
        gam, bet = sb("gam", [P, D]), sb("bet", [P, D])
        obias, boB, bvB = sb("obias", [P, D]), sb("boB", [P, D]), sb("bvB", [P, D])
        g1, be1, g2, be2 = (sb(n, [P, D]) for n in ("g1", "be1", "g2", "be2"))
        bgB, b2B = sb("bgB", [P, E]), sb("b2B", [P, E, D])
        slotC = sb("slotC", [P, D])
        ident, iota = sb("ident", [P, P]), sb("iota", [S, T])
        upper = sb("upper", [S, S])
        earlier = sb("earlier", [P, E, E])
        sgn, off = sb("sgn", [P, 1]), sb("off", [P, 1])
        mhalf, half = sb("mhalf", [P, 2]), sb("half", [P, 2 * FCH])
        idT = sb("idT", [S, 2, B])
        kmask, slot, val, ttv = sb("kmask", [S, 2, B]), sb("slot", [S, B + 2]), sb("val", [S, B + 2]), sb("ttv", [S, B + 2])
        pref = sb("pref", [S, 2, B])
        post, ttd = sb("post", [S, D]), sb("ttd", [S, D])
        onehot, embR = sb("onehot", [S, 2, T]), sb("embR", [S, 2, XW])
        emb = sb("emb", [P, 2, XW])
        idxw, idxk = sb("idxw", [HALF, 2], i32), sb("idxk", [P, 1], i32)
        rows = sb("rows", [P, 2, D])
        entg, entT = sb("entg", [P, D_ENT]), sb("entT", [D_ENT, P])
        coef = sb("coef", [P, 2])
        h0, h1, h1keep = (sb(n, [P, 2, D]) for n in ("h0", "h1", "h1keep"))
        bD, xD = (sb(n, [P, 2, 2 * P]) for n in ("bD", "xD"))
        aD = xD
        xT = sb("xT", [P, 2 * NT])
        aT = xT
        qt, kt = sb("qt", [P, QCH * NT]), sb("kt", [P, QCH * NT])
        NM, NR = HEADS * NT, HEADS * T
        hid = qt[:, :].rearrange("p (a k n) -> p a k n", a=2, k=KCH)
        vp = sb("vp", [P, 2, HEADS * D])
        v2a = sb("v2a", [P, HEADS, D])
        with nc.sbuf_tensor("v2b", [P, HEADS, D], f32) as v2b:
            v2 = (v2a, v2b)
        xH, xL = (sb(n, [P, 2 * NT], f32r) for n in ("xH", "xL"))
        bT = sb("bT", [P, 2 * NT])
        bH, bL, aH, aL = xH, xL, xH, xL
        oflat = vp[:, :, :].rearrange("p s n -> p (s n)")
        oT = oflat[:, 0:NM].rearrange("p (c n) -> p c n", c=HEADS)
        oR = oflat[:, NM:NM + NR].rearrange("p (c n) -> p c n", c=HP)
        prob = sb("prob", [P, 4, 4, T])
        probT = sb("probT", [P, 2, 4, T])
        fqT, fkT = (kt[:, k * FCH * NT:(k + 1) * FCH * NT].rearrange("p (c n) -> p c n", c=FCH) for k in range(2))
        fval = sb("fval", [P, 2, D])
        pflat = probT[:, :, :, :].rearrange("p a b c -> p (a b c)")
        fo = pflat[:, 0:2 * D].rearrange("p (s n) -> p s n", s=2)
        foT = pflat[:, 2 * D:2 * D + 2 * NT].rearrange("p (c n) -> p c n", c=2)
        fwo = fo
        pre = sb("pre", [P, 2, D])
        ff, res = pre, xD[:, :, 0:D]
        st, mv, ve, rstd = sb("st", [P, 2, 6]), sb("mv", [P, 2, 2]), sb("ve", [P, 2]), sb("rstd", [P, 2])
        nmax, asum, arec = sb("nmax", [P, 4, 4]), sb("asum", [P, 4, 4]), sb("arec", [P, 4, 4])
        fst = sb("fst", [P, 2, 2 * FCH, 6])
        fd, fw, fm2 = (sb(n, [P, 2 * FCH]) for n in ("fd", "fw", "fm2"))
        fmax, fvar, fsd = (sb(n, [P, 2, 2 * FCH]) for n in ("fmax", "fvar", "fsd"))
        fden, finv, fsc, fnb = (sb(n, [P, 4, 2 * FCH]) for n in ("fden", "finv", "fsc", "fnb"))
        fsum, frec = sb("fsum", [P, 2, FHEADS]), sb("frec", [P, 2, FHEADS])
        gl, gs, gx, gp, grk, comb = (sb(n, [P, 2, E]) for n in ("gl", "gs", "gx", "gp", "grk", "comb"))
        gm, gsum, grec = sb("gm", [P, 2]), sb("gsum", [P, 2]), sb("grec", [P, 2])
        ggt, gge = sb("ggt", [P, 2, E, E]), sb("gge", [P, 2, E, E])
        def part(t, start, rows_, *dims):
            flat = t if len(t.shape) == 2 else t.rearrange("p a b -> p (a b)") if len(t.shape) == 3 else \
                t.rearrange("p a b c -> p (a b c)")
            n = 1
            for d in dims:
                n *= d
            v = flat[0:rows_, start:start + n]
            return v if len(dims) == 1 else v.rearrange("p (a b) -> p a b", a=dims[0])

        brow = part(probT[:, :, :, :], 0, 2 * QCH, P)
        fstage = part(prob[:, :, :, :], 0, P, 8 * D)
        kwA, kwB = part(prob[:, :, :, :], 8 * D, P, D_ENT), part(prob[:, :, :, :], 8 * D + D_ENT, R, D_ENT)
        b1row = part(prob[:, :, :, :], 8 * D + 2 * D_ENT, E * KCH, P)
        fqk = (part(probT[:, :, :, :], P, P, 2 * D), part(probT[:, :, :, :], P + 2 * D, P, 2 * D), fvo[:, 0, :], fvo[:, 1, :])
        wgrow = part(h1[:, :, :], 0, E, D)
        ids_f, ids_i = part(h1[:, :, :], D, B, 2, S), part(h1keep[:, :, :], 0, B, 2, S).bitcast(i32)
        tt0, ones = part(h1keep[:, :, :], 2 * S, S, D), part(xD[:, :, :], 0, P, P)
        qvA = [kt[:, k * HEADS * D:(k + 1) * HEADS * D] for k in range(2)]
        qvB = [v2[1 - k][0:R, :, :].rearrange("p g n -> p (g n)") for k in range(2)]
        w1A, w1B = part(w2[:, :, :], 0, P, E * FF), part(w2[:, :, :], E * FF, R, E * FF // 2)
        gsc = sb("gsc", [P, 1])

        unit = [ctx.enter_context(nc.psum_tensor(f"unit{n}", [P, 4, T], f32)) for n in range(4)]
        bank = [ctx.enter_context(nc.psum_tensor(f"bank{n}", [P, 512], f32)) for n in range(3)]
        acc = ctx.enter_context(nc.psum_tensor("acc", [P, 512], f32))

        def place(at, name):
            return bank[DRAINS[at[0]].index(name) % 3]

        def unit_of(n):
            return unit[n % 4]

        filled, drained = sem("filled"), sem("drained")
        acc_filled, acc_drained = sem("acc_filled"), sem("acc_drained")
        ld_ids, ld_tok, ld_small, ld_w2 = sem("ld_ids"), sem("ld_tok"), sem("ld_small"), sem("ld_w2")
        ld_rows, ld_w1 = sem("ld_rows"), (sem("ld_w1_first"), sem("ld_w1_second"))
        ld_attn, ld_split, v_moved, v_ready = sem("ld_attn"), sem("ld_split"), (sem("v_moved0"), sem("v_moved1")), sem("v_ready")
        stats_seen = sem("stats_seen")
        zeroed, const_ready = sem("zeroed"), sem("const_ready")
        ids_ready, mask_ready = sem("ids_ready"), sem("mask_ready")
        w1_hi, w1_split = sem("w1_hi"), sem("w1_split")
        pro_step = sem("pro_step")
        onehot_ready, idx_ready, gather_go, got_words, got_ents = (sem(n) for n in ("onehot_ready", "idx_ready", "gather_go", "got_words", "got_ents"))
        index_step, tok_step, attn_step, ftail_step, moe_step, ffn_step = (
            sem(n) for n in ("index_step", "tok_step", "attn_step", "ftail_step", "moe_step", "ffn_step"))
        var_ready = {k: sem(f"var_{k}") for k in "tabxo"}
        rstd_ready = {k: sem(f"rstd_{k}") for k in "tabxo"}
        aD_ready, bD_ready, xD_ready = sem("aD_ready"), sem("bD_ready"), sem("xD_ready")
        a_split, b_split, x_split = sem("a_split"), sem("b_split"), sem("x_split")
        qv_hi, q_split, v_split = sem("qv_hi"), sem("q_split"), sem("v_split")
        a_scores, a_max, a_exp, a_prob, a_turned, a_probT = (sem(n) for n in ("a_scores", "a_max", "a_exp", "a_prob", "a_turned", "a_probT"))
        f_scores, f_var, f_sd, f_scale, f_exp, f_turned, f_probT = (
            sem(n) for n in ("f_scores", "f_var", "f_sd", "f_scale", "f_exp", "f_turned", "f_probT"))
        fval_ready, fo_ready = sem("fval_ready"), sem("fo_ready")
        gate_ready, gate_shift, gate_exp = sem("gate_ready"), sem("gate_shift"), sem("gate_exp")
        out_ready, stored = sem("out_ready"), sem("stored")

        block = ctx.enter_context(nc.Block())

        TOK, ROWS, SMALL = 13, 6, 26

        @block.sync
        def _(sp):
            def tok(dst, src):
                sp.dma_start(dst, src).then_inc(ld_tok, 16)

            def bias_row(dst, src):
                sp.dma_start(dst, src).then_inc(ld_rows, 16)

            def row(dst, src):
                sp.dma_start(dst, src).then_inc(ld_small, 16)

            def bcast(dst, src):
                row(dst, src[None, :].to_broadcast([P, src.shape[0]]))

            def load(dst, src):
                sp.dma_start(dst, src).then_inc(ld_attn, 16)

            def load_blocks(dst, src, ready):
                dst = dst.rearrange("r (p n) -> r p n", n=2 * D)
                src = src.rearrange("r (p j n) -> r p j n", j=2, n=D)
                sp.dma_start(dst[:, :, 0:D], src[:, :, 0, :]).then_inc(ready, 16)
                sp.dma_start(dst[:, :, D:2 * P], src[:, :, 1, P:D]).then_inc(ready, 16)
                sp.dma_start(dst[:, :, 2 * P:3 * P], src[:, :, 1, 0:P]).then_inc(ready, 16)

            sp.dma_start(ids_i[:, 0, :], x).then_inc(ld_ids, 16)
            sp.dma_start(ids_i[:, 1, :], mask).then_inc(ld_ids, 16)
            tok(kwA[:, :], ke_w[0:P, :])
            tok(kwB[:, :], ke_w[P:D, :])
            tok(post[:, :], pos_emb[0:S, :])
            tok(tt0[:, :], tt_emb[0:1, :].to_broadcast([S, D]))
            tok(ttd[:, :], tt_emb[1:2, :].to_broadcast([S, D]))
            tok(slotC[0:HALF, :], pos_emb[0:HALF, :])
            tok(slotC[HALF:P, :], ke_b[None, :].to_broadcast([HALF, D]))
            tok(rows[0:HALF, 0, :], tt_emb[1:2, :].to_broadcast([HALF, D]))
            for lo, g, b in ((0, w_gamma, w_beta), (HALF, k_gamma, k_beta)):
                tok(gam[lo:lo + HALF, :], g[None, :].to_broadcast([HALF, D]))
                tok(bet[lo:lo + HALF, :], b[None, :].to_broadcast([HALF, D]))
            tok(obias[:, :], b_proj[None, :].to_broadcast([P, D]))
            qk_b = b_qkv[0:2 * HEADS * D].rearrange("(a j n) -> a j n", j=2, n=D)
            bias_row(brow[0:HEADS, :], qk_b[:, 0, 0:P])
            bias_row(brow[HEADS:2 * HEADS, 0:R], qk_b[:, 0, P:D])
            bias_row(brow[HEADS:2 * HEADS, R:P], qk_b[:, 1, P:D])
            bias_row(brow[2 * HEADS:3 * HEADS, :], qk_b[:, 1, 0:P])
            bias_row(b1row[:, :], b1.rearrange("e (c p) -> (e c) p", p=P))
            bias_row(wgrow[:, :], Wg)
            w = [W_qkv[:, m * HEADS * D:(m + 1) * HEADS * D] for m in range(3)]
            for t, r in ((qvA, slice(0, P)), (qvB, slice(P, D))):
                load_blocks(t[0], w[0][r], ld_split)
                sp.dma_start(t[1], w[2][r]).then_inc(ld_split, 16)
            load_blocks(wk[:, :], w[1][0:P, :], ld_attn)
            half_k = HEADS * D // 2
            for k in range(2):
                load_blocks(wkR[R * k:R * k + R, :], w[1][P:D, k * half_k:(k + 1) * half_k], ld_attn)
            load(wp[:, :, :], W_proj.rearrange("(c r) n -> r c n", r=D)[0:P])
            for j in range(2):
                load(wpR[R * j:R * j + R, :, :], W_proj.rearrange("(p j r) n -> j r p n", j=2, r=D)[j, P:D])
            row(bv2[:, :], b_qkv[2 * HEADS * D:3 * HEADS * D][None, :].to_broadcast([GT, HEADS * D]))
            for m, w in enumerate((Wq, Wk, Wv, Wo)):
                row(fstage[:, m * 2 * D:m * 2 * D + D], w[0:P, :])
                row(fstage[0:R, m * 2 * D + D:(m + 1) * 2 * D], w[P:D, :])
            for dst, src in ((boB, bo), (bvB, bv), (g1, ln1_g), (be1, ln1_b), (g2, ln2_g),
                             (be2, ln2_b), (bgB, bg), (gsc, gamma)):
                bcast(dst[:, :], src)
            row(b2B[:, :, :], b2[None, :, :].to_broadcast([P, E, D]))
            sp.wait_ge(zeroed, 2)
            for dst, src in ((fqb, bq), (fkb, bk)):
                for s in range(4):
                    sp.dma_start(dst[32 * s:32 * s + HD, :], src.rearrange("(c s d) -> s d c", s=4, d=HD)[s],
                                 allow_slow_non_contiguous=True).then_inc(ld_small, 16)
            def load_w1_rest(k):
                sp.dma_start(w1B.rearrange("p (e n) -> p e n", e=2), W1[2 * k:2 * k + 2, P:D, :].rearrange("e k n -> k e n"))\
                  .then_inc(ld_w1[k], 16)

            sp.dma_start(w1A.rearrange("p (e n) -> p e n", e=E), W1[:, 0:P, :].rearrange("e k n -> k e n")).then_inc(ld_w1[0], 16)
            load_w1_rest(0)
            sp.sem_inc(stored, 16)
            out_v = out.rearrange("(j s) t d -> j t s d", s=2)

            def move_values(at):
                for s in range(2):
                    sp.wait_ge(drained, drain_no(at, VU[3 * s + 2]) + 1)
                    for g in range(HEADS):
                        sp.dma_start(v2[s][:, g, :], vp[g * GT:(g + 1) * GT, s, :]).then_inc(v_moved[s], 16)

            def store(j):
                sp.wait_ge(out_ready, j + 1)
                sp.dma_start(out_v[ds(j, 1)].rearrange("a t s d -> t (a s) d"), res).then_inc(stored, 16)

            move_values(("first", 0))
            sp.wait_ge(w1_split, 2)
            load_w1_rest(1)
            move_values(("peel", 0))
            sp.wait_ge(w1_split, 3)
            sp.dma_start(w2[:, :, :], W2.rearrange("e (c p) n -> p (e c) n", p=P)).then_inc(ld_w2, 16)
            with sp.Fori(1, PAIRS - 1, 1) as i:
                move_values(("loop", i - 1))
                store(i - 1)
            store(PAIRS - 2)
            store(PAIRS - 1)
            sp.wait_ge(stored, 16 * (PAIRS + 1))

        @block.gpsimd
        def _(pool):
            pool.memset(fqb[:, :], 0.0).then_inc(zeroed, 1)
            pool.memset(fkb[:, :], 0.0).then_inc(zeroed, 1)
            for t in (fqH, fqL, fqS, fkH, fkL, fkS):
                pool.memset(t[:, :].bitcast(f32), 0.0).then_inc(zeroed, 1)
            pool.memset(ones[:, :], 1.0).then_inc(zeroed, 1)
            pool.memset(ident[:, :], 0.0).then_inc(zeroed, 1)
            pool.wait_ge(zeroed, 10)
            pool.affine_select(out=ident[:, :], in_=ident[:, :], compare_op=ALU.not_equal, fill=1.0, base=0,
                               pattern=[[-1, P]], channel_multiplier=1).then_inc(const_ready, 1)
            pool.affine_select(out=upper[:, :], in_=ones[0:S, 0:S], compare_op=ALU.is_ge, fill=0.0, base=0,
                               pattern=[[1, S]], channel_multiplier=-1).then_inc(const_ready, 1)
            pool.iota(iota[:, :], pattern=[[1, T]], base=0, channel_multiplier=0,
                      allow_small_or_imprecise_dtypes=True).then_inc(const_ready, 1)
            pool.memset(earlier[:, :, :], 0.0).then_inc(const_ready, 1)
            pool.memset(mhalf[:, :], -0.5).then_inc(const_ready, 1)
            pool.memset(half[:, :], 0.5).then_inc(const_ready, 1)

            def gathers(i):
                pool.wait_ge(idx_ready, i + 1)
                pool.sem_inc(gather_go, 1)
                for s in range(2):
                    pool.indirect_dma_start(out=rows[0:HALF, s, :], out_offset=None, in_=word_emb,
                                            in_offset=bass.IndirectOffsetOnAxis(ap=idxw[:, s:s + 1], axis=0))\
                        .then_inc(got_words, 16)
                pool.indirect_dma_start(out=entg[:, :], out_offset=None, in_=ent_emb,
                                        in_offset=bass.IndirectOffsetOnAxis(ap=idxk[:, 0:1], axis=0))\
                    .then_inc(got_ents, 16)

            def inverse_root(kind, i):
                pool.wait_ge(var_ready[kind], i + 1)
                pool.tensor_tensor(out=rstd[:, :], in0=ve[:, :], in1=mhalf[:, :], op=ALU.pow)\
                    .then_inc(rstd_ready[kind], 1)

            def value_bias(i, s):
                pool.wait_ge(v_moved[s], 16 * HEADS * (i + 1))
                v = v2[s][:, :, :]
                pool.tensor_tensor(out=v, in0=v, in1=bv2[:, None, :].to_broadcast([P, HEADS, D]), op=ALU.add)\
                    .then_inc(v_ready, 1)

            def roots(i):
                for k in range(4):
                    pool.wait_ge(f_var, 4 * i + k + 1)
                    pool.tensor_tensor(out=fsd[:, k % 2, :], in0=fvar[:, k % 2, :], in1=half[:, :], op=ALU.pow).then_inc(f_sd, 1)

            gathers(0)
            inverse_root("t", 0)
            inverse_root("a", 0)
            pool.wait_ge(qv_hi, 2)
            pool.tensor_tensor(out=wvL[:, :], in0=qvA[1], in1=wvH[:, :].bitcast(f32), op=ALU.subtract)\
                .then_inc(v_split, 1)
            pool.wait_ge(v_split, 1)
            pool.tensor_tensor(out=wvS[R:P, :], in0=qvB[1], in1=wvS[0:R, :].bitcast(f32), op=ALU.subtract)\
                .then_inc(v_split, 1)
            pool.wait_ge(ld_small, 16 * SMALL)
            gathers(1)
            value_bias(0, 0)
            value_bias(0, 1)
            inverse_root("b", 0)
            inverse_root("t", 1)
            inverse_root("a", 1)
            roots(0)
            value_bias(1, 0)
            with pool.Fori(1, PAIRS - 1, 1) as i:
                inverse_root("x", i - 1)
                value_bias(i, 1)
                gathers(i + 1)
                inverse_root("b", i)
                inverse_root("t", i + 1)
                inverse_root("a", i + 1)
                roots(i)
                inverse_root("o", i - 1)
                value_bias(i + 1, 0)
            inverse_root("x", PAIRS - 2)
            value_bias(PAIRS - 1, 1)
            inverse_root("b", PAIRS - 1)
            roots(PAIRS - 1)
            inverse_root("o", PAIRS - 2)
            inverse_root("x", PAIRS - 1)
            inverse_root("o", PAIRS - 1)

        @block.scalar
        def _(act):
            def drain(at, name, *ops):
                act.wait_ge(filled, drain_no(at, name) + 1)
                for dst, src in ops[:-1]:
                    act.activation(dst, src, ACT.Copy)
                act.activation(*ops[-1], ACT.Copy).then_inc(drained, 1)

            W = ("ids", 0)
            drain(W, "ids", (idT[:, :, :], place(W, "ids")[0:S, 0:2 * B].rearrange("p (a b) -> p a b", a=2)))
            drain(W, "prefix", (pref[:, :, :], place(W, "prefix")[0:S, 0:2 * B].rearrange("p (a b) -> p a b", a=2)))
            drain(W, "ke_w", (kewT[:, :], place(W, "ke_w")[0:D_ENT, 0:D]))

            def entities(at, i):
                drain(at, "ent", (entT[:, :], place(at, "ent")[0:D_ENT, 0:P]))

            def projected(at, i):
                act.wait_ge(filled, drain_no(at, "proj") + 1)
                u = place(at, "proj")
                act.activation(rows[HALF:P, 0, :], u[HALF:P, 0:D], ACT.Copy, scale=emb[HALF:P, 0, D + 1:D + 2])
                act.activation(rows[HALF:P, 1, :], u[HALF:P, D:2 * D], ACT.Copy, scale=emb[HALF:P, 1, D + 1:D + 2])\
                   .then_inc(drained, 1)

            def whole(at, name, dst):
                drain(at, name, (dst, place(at, name)[:, :]))

            def index(at):
                drain(at, "index", (emb[:, :, :].rearrange("p s n -> p (s n)"), place(at, "index")[:, 0:2 * XW]))

            def projected_rows(at, m, lo, hi):
                t = (qt, kt)[m]
                main = t[:, 0:NM].rearrange("p (n c) -> p c n", c=HEADS)
                rest = t[:, NM:NM + NR].rearrange("p (n c) -> p c n", c=HEADS)
                for n in range(lo, hi):
                    name = (QU, KU)[m][n]
                    u = place(at, name)
                    act.wait_ge(filled, drain_no(at, name) + 1)
                    for k in range(2):
                        p, x = divmod(2 * ORDER[n] + k, 3)
                        col = slice(x * HEADS + m * HP + p, x * HEADS + m * HP + p + 1)
                        if x != 1:
                            ins = act.activation(main[:, 2 * p + x // 2, :], u[:, k * NT:(k + 1) * NT], ACT.Identity,
                                                 bias=qkbias[:, col])
                            continue
                        for j in range(2):
                            r = slice(R * j, R * j + R)
                            for s in range(2):
                                ins = act.activation(rest[R * s:R * s + R, 2 * p + j, :],
                                                     u[r, k * NT + s * T:k * NT + (s + 1) * T], ACT.Identity,
                                                     bias=qkbias[r, col])
                    ins.then_inc(drained, 1)

            def values(at, n):
                whole(at, VU[n], vp[:, n // 3, n % 3 * 512:(n % 3 + 1) * 512])

            def outputs(at, s):
                for u in (2 * s, 2 * s + 1):
                    drain(at, f"om{u}", (oT[:, :, u * NT // 4:(u + 1) * NT // 4],
                                         place(at, f"om{u}")[:, :].rearrange("p (n c) -> p c n", c=HEADS)))
                drain(at, f"or{s}", (oR[:, :, s * T:(s + 1) * T],
                                     place(at, f"or{s}")[:, :].rearrange("p (n c) -> p c n", c=HP)))

            def attn_exp(i, u):
                act.wait_ge(a_max, 4 * i + u + 1)
                for k in range(4):
                    act.activation(prob[:, u, k, :], unit_of(u)[:, k, :], ACT.Exp, bias=nmax[:, u, k:k + 1],
                                   accum_out=asum[:, u, k:k + 1]).then_inc(a_exp, 1)

            def ffn_exp(i, u):
                k, s = u // 2, u % 2
                act.wait_ge(f_scale, 4 * i + k + 1)
                for c in range(FCH):
                    n = FCH * s + c
                    act.activation(prob[:, u % 4, c, :], unit_of(u)[:, c, :], ACT.Exp, bias=fnb[:, k, n:n + 1],
                                   scale=fsc[:, k, n:n + 1], accum_out=fsum[:, s, 4 * c + k:4 * c + k + 1])\
                       .then_inc(f_exp, 1)

            def expert_up(at, n):
                u = place(at, UP[n])
                act.wait_ge(filled, drain_no(at, UP[n]) + 1)
                for k in range(2):
                    c = 2 * n + k
                    ins = act.activation(hid[:, c // KCH % 2, c % KCH, :], u[:, k * NT:(k + 1) * NT], ACT.Relu,
                                         bias=b1c[:, c:c + 1])
                ins.then_inc(drained, 1)

            def ffn_projections(at):
                for c in range(FCH):
                    u = place(at, f"qk{c}")
                    act.wait_ge(filled, drain_no(at, f"qk{c}") + 1)
                    act.activation(fqT[:, c, :], u[:, 0:NT], ACT.Identity, bias=fqb[:, c:c + 1], scale=qscale[:, 0:1])
                    act.activation(fkT[:, c, :], u[:, NT:2 * NT], ACT.Identity, bias=fkb[:, c:c + 1])\
                       .then_inc(drained, 1)

            def ffn_value(at):
                drain(at, "fval", (fval[:, :, :].rearrange("p s n -> p (s n)"), place(at, "fval")[:, 0:2 * D]))

            def ffn_out_turned(at):
                u = place(at, "attnT")
                drain(at, "attnT", (foT[:, 0, :], u[:, 0:NT]), (foT[0:R, 1, :], u[0:R, NT:2 * NT]))

            def ffn_out(at):
                drain(at, "wo", (fwo[:, :, :].rearrange("p s n -> p (s n)"), place(at, "wo")[:, 0:2 * D]))

            def gate_exps(j):
                act.wait_ge(gate_shift, j + 1)
                act.activation(gx[:, :, :], gs[:, :, :], ACT.Exp).then_inc(gate_exp, 1)

            at = ("first", 0)
            index(at)
            entities(at, 0)
            projected(at, 0)
            act.wait_ge(ld_split, 16 * 8)
            for k, (H, St) in enumerate(((wqH, wqS), (wvH, wvS))):
                act.activation(H[:, :], qvA[k], ACT.Copy)
                act.activation(St[0:R, :], qvB[k], ACT.Copy).then_inc(qv_hi, 1)
            u, nb = place(at, "small"), 2 * QCH
            drain(at, "small", (b1c[:, :], u[:, 0:nb]), (qkbias[:, :], u[:, nb:2 * nb]),
                  (wgT[:, 0:E], u[:, 2 * nb:2 * nb + E]), (wgT[0:R, E:2 * E], u[0:R, 2 * nb + E:2 * nb + 2 * E]))
            whole(at, "aT", aT[:, :])
            projected_rows(at, 0, 0, 6)
            for n in range(6):
                values(at, n)
            for m, name in enumerate(("fq", "fk", "fv", "fo")):
                u = place(at, name)
                drain(at, name, (fqk[m][:, 0:D], u[:, 0:D]), (fqk[m][0:R, D:2 * D], u[0:R, D:2 * D]))

            def w1_parts(k):
                act.wait_ge(ld_w1[k], 16 * (2 - k))
                if k == 0:
                    act.activation(w1H[:, :], w1A, ACT.Copy).then_inc(w1_hi, 1)
                act.activation(w1S[0:R, k * E * FF // 2:(k + 1) * E * FF // 2], w1B, ACT.Copy).then_inc(w1_hi, 1)

            def step(at, i, full, ahead=True):
                projected_rows(at, 1, 0, 1)
                if full:
                    ffn_out_turned(at)
                projected_rows(at, 1, 1, 3)
                if full:
                    ffn_out(at)
                else:
                    index(at)
                projected_rows(at, 1, 3, 6)
                if full and ahead:
                    index(at)
                for u in range(4):
                    attn_exp(i, u)
                act.wait_ge(v_moved[1], 16 * HEADS * (i + 1))
                outputs(at, 0)
                outputs(at, 1)
                if not full:
                    w1_parts(0)
                if full:
                    whole(at, "xT", xT[:, :])
                if ahead:
                    entities(at, i + 1)
                if full:
                    for n in range(3):
                        expert_up(at, n)
                    if ahead:
                        projected(at, i + 1)
                    gate_exps(i - 1)
                    for n in range(3, 6):
                        expert_up(at, n)
                whole(at, "bT", bT[:, :])
                if full:
                    for n in range(6, 9):
                        expert_up(at, n)
                    ffn_value(at)
                    for n in range(9, 12):
                        expert_up(at, n)
                    ffn_projections(at)
                    if ahead:
                        whole(at, "aT", aT[:, :])
                else:
                    projected(at, i + 1)
                    ffn_value(at)
                    ffn_projections(at)
                    whole(at, "aT", aT[:, :])
                if ahead:
                    projected_rows(at, 0, 0, 1)
                for u in range(FU):
                    ffn_exp(i, u)
                    if ahead and u == 1:
                        projected_rows(at, 0, 1, 3)
                    if ahead and u == 3:
                        projected_rows(at, 0, 3, 6)
                        values(at, 0)
                    if ahead and u == 5:
                        values(at, 1)
                        values(at, 2)
                        values(at, 3)
                if ahead:
                    values(at, 4)
                    values(at, 5)
                if not full:
                    w1_parts(1)

            step(("peel", 0), 0, False)
            with act.Fori(1, PAIRS - 1, 1) as i:
                step(("loop", i - 1), i, True)
            step(("final", 0), PAIRS - 1, True, ahead=False)
            at = ("last", 0)
            ffn_out_turned(at)
            ffn_out(at)
            whole(at, "xT", xT[:, :])
            for n in range(12):
                expert_up(at, n)
                if n == 2:
                    gate_exps(PAIRS - 1)

        @block.vector
        def _(dve):
            one = Steps(dve, pro_step, 0, 33)

            def link(ins):
                one.did(ins)
                one.wait()

            dve.wait_ge(ld_ids, 32)
            dve.tensor_copy(ids_f[:, :, :], ids_i[:, :, :]).then_inc(ids_ready, 1)
            dve.wait_ge(drained, drain_no(("ids", 0), "ids") + 1)
            link(dve.tensor_scalar(kmask[:, 0, :], idT[:, 0, :], 0.0, None, ALU.is_gt))
            link(dve.scalar_tensor_tensor(out=kmask[:, 0, :], in0=idT[:, 0, :], scalar=float(VOCAB),
                                          in1=kmask[:, 0, :], op0=ALU.is_lt, op1=ALU.mult))
            dve.tensor_scalar(kmask[:, 1, :], idT[:, 0, :], float(VOCAB), None, ALU.is_ge).then_inc(mask_ready, 1)
            dve.wait_ge(mask_ready, 1)
            link(dve.memset(val[:, :], 0.0))
            link(dve.memset(slot[:, :], -1.0))
            link(dve.memset(ttv[:, :], 0.0))
            link(dve.memset(embR[:, :, :], 1.0))
            link(dve.scalar_tensor_tensor(out=val[:, 0:B], in0=kmask[:, 1, :], scalar=-float(VOCAB), in1=idT[:, 0, :],
                                          op0=ALU.mult, op1=ALU.add))
            link(dve.tensor_copy(ttv[:, 0:B], idT[:, 1, :]))
            dve.memset(sgn[0:HALF, :], -1.0)
            dve.memset(sgn[HALF:P, :], 1.0)
            dve.memset(off[0:HALF, :], 1.0)
            link(dve.memset(off[HALF:P, :], 0.0))
            dve.wait_ge(drained, drain_no(("ids", 0), "prefix") + 1)
            link(dve.scalar_tensor_tensor(out=kmask[:, :, :], in0=pref[:, :, :], scalar=float(HALF) + 0.5,
                                          in1=kmask[:, :, :], op0=ALU.is_lt, op1=ALU.mult))
            link(dve.tensor_scalar(pref[:, 1, :], pref[:, 1, :], float(HALF), None, ALU.add))
            link(dve.tensor_tensor(out=pref[:, :, :], in0=pref[:, :, :], in1=kmask[:, :, :], op=ALU.mult))
            link(dve.tensor_tensor(out=slot[:, 0:B], in0=pref[:, 0, :], in1=pref[:, 1, :], op=ALU.add))
            link(dve.tensor_scalar(slot[:, 0:B], slot[:, 0:B], -1.0, None, ALU.add))
            dve.wait_ge(ld_tok, 16 * TOK)
            dve.wait_ge(zeroed, 10)
            dve.wait_ge(const_ready, 6)
            for e in range(1, E):
                link(dve.memset(earlier[:, e, 0:e], 1.0))
            link(dve.tensor_tensor(out=ttd[:, :], in0=ttd[:, :], in1=tt0[:, :], op=ALU.subtract))
            link(dve.tensor_tensor(out=post[:, :], in0=post[:, :], in1=tt0[:, :], op=ALU.add))
            link(dve.tensor_tensor(out=slotC[0:HALF, :], in0=slotC[0:HALF, :], in1=rows[0:HALF, 0, :], op=ALU.add))

            def build_onehot(i):
                k = Steps(dve, index_step, i, 6)
                for s in range(2):
                    col = ds(2 * i + s, 1)
                    k.did(dve.tensor_scalar(onehot[:, s, :], iota[:, :], slot[:, col], None, ALU.is_equal))
                    k.did(dve.scalar_tensor_tensor(out=embR[:, s, 0:D], in0=ttd[:, :], scalar=ttv[:, col],
                                                   in1=post[:, :], op0=ALU.mult, op1=ALU.add))
                    k.did(dve.tensor_copy(embR[:, s, D:D + 1], val[:, col]))
                k.end()
                k.wait()
                dve.sem_inc(onehot_ready, 1)

            def build_index(at, i):
                dve.wait_ge(drained, drain_no(at, "index") + 1)
                dve.tensor_copy(idxw[:, :], emb[0:HALF, :, D:D + 1].rearrange("p s o -> p (s o)"))
                for s in range(2):
                    ins = dve.tensor_scalar(idxk[s * HALF:(s + 1) * HALF, :], emb[HALF:P, s, D:D + 1],
                                            float(N_ENT - 1), None, ALU.min)
                ins.then_inc(idx_ready, 1)

            def normalise(k, kind, i, src, dst, eps):
                for s in range(2):
                    k.did(dve.bn_stats(st[:, s, :], src[:, s, :]))
                k.wait()
                dve.sem_inc(stats_seen, 1)
                for s in range(2):
                    k.did(dve.bn_aggr(mv[:, s, :], st[:, s, :]))
                k.wait()
                dve.tensor_scalar(ve[:, :], mv[:, :, 1:2].rearrange("p s o -> p (s o)"), eps, None, ALU.add)\
                   .then_inc(var_ready[kind], 1)
                dve.wait_ge(rstd_ready[kind], i + 1)
                for s in range(2):
                    k.did(dve.tensor_scalar(dst[:, s, 0:D], src[:, s, :], mv[:, s, 0:1], rstd[:, s:s + 1],
                                            ALU.subtract, ALU.mult))
                k.wait()

            def over(v):
                return v[:, None, :].to_broadcast([P, 2, D])

            def affine(k, t, g, b):
                k.did(dve.tensor_tensor(out=t, in0=t, in1=over(g), op=ALU.mult))
                k.wait()
                k.did(dve.tensor_tensor(out=t, in0=t, in1=over(b), op=ALU.add))
                k.wait()

            def twice(t, ready):
                dve.tensor_copy(t[:, :, D:2 * P], t[:, :, P:D]).then_inc(ready, 1)

            def split(at, name, src, H, L, ready, n):
                dve.wait_ge(drained, drain_no(at, name) + 1)
                dve.tensor_copy(H[:, :], src[:, :]).then_inc(ready, 1)
                dve.wait_ge(ready, 2 * n + 1)
                dve.tensor_tensor(out=L[:, :], in0=src[:, :], in1=H[:, :].bitcast(f32), op=ALU.subtract).then_inc(ready, 1)

            def embed(k, at, i):
                dve.wait_ge(drained, drain_no(at, "proj") + 1)
                dve.wait_ge(got_words, 32 * (i + 1))
                k.did(dve.tensor_tensor(out=rows[:, :, :], in0=rows[:, :, :], in1=emb[:, :, 0:D], op=ALU.add))
                k.did(dve.tensor_scalar(coef[:, :], emb[:, :, D + 1:D + 2].rearrange("p s o -> p (s o)"), sgn[:, 0:1],
                                        off[:, 0:1], ALU.mult, ALU.add))
                k.wait()
                for s in range(2):
                    k.did(dve.scalar_tensor_tensor(out=rows[:, s, :], in0=slotC[:, :], scalar=coef[:, s:s + 1],
                                                   in1=rows[:, s, :], op0=ALU.mult, op1=ALU.add))
                k.wait()
                normalise(k, "t", i, rows, h0, EPS_TOK)
                affine(k, h0[:, :, :], gam, bet)

            def attn_input(k, i):
                normalise(k, "a", i, h0, aD, EPS)
                twice(aD, aD_ready)
                k.did(dve.tensor_tensor(out=h0[:, :, :], in0=h0[:, :, :], in1=over(obias), op=ALU.add))
                k.wait()
                k.did(dve.tensor_copy(coef[:, 0:1], sgn[:, 0:1]))
                k.end()

            def attn_max(i, u):
                dve.wait_ge(a_scores, 4 * i + u + 1)
                dve.tensor_reduce(nmax[:, u, :], unit_of(u)[:, :, :], AX.X, ALU.max, negate=True).then_inc(a_max, 1)

            def attn_norm(k, i, u):
                dve.wait_ge(a_exp, 16 * i + 4 * u + 4)
                k.did(dve.reciprocal(arec[:, u, :], asum[:, u, :]))
                k.wait()
                for n in range(4):
                    ins = dve.tensor_scalar(prob[:, u, n, :], prob[:, u, n, :], arec[:, u, n:n + 1], D ** -0.5,
                                            ALU.mult, ALU.mult)
                ins.then_inc(a_prob, 1)

            def attn_turn(i, u):
                dve.wait_ge(a_turned, 4 * i + u + 1)
                dve.tensor_copy(probT[:, u % 2, :, :], unit_of(u)[:, :, :]).then_inc(a_probT, 1)

            def attn_out(k, at, i):
                dve.wait_ge(acc_filled, sum_no(at, "attn") + 1)
                dve.tensor_tensor(out=h1[:, :, :].rearrange("p s n -> p (s n)"), in0=acc[:, 0:2 * D],
                                  in1=h0[:, :, :].rearrange("p s n -> p (s n)"), op=ALU.add).then_inc(acc_drained, 1)
                dve.wait_ge(acc_drained, sum_no(at, "attn") + 1)
                normalise(k, "b", i, h1, bD, EPS)
                twice(bD, bD_ready)

            def ffn_tail(at, j):
                k = Steps(dve, ftail_step, j, 10)
                k.did(dve.tensor_tensor(out=pre[:, :, :], in0=bD[:, :, 0:D], in1=over(boB), op=ALU.add))
                k.wait()
                dve.wait_ge(drained, drain_no(at, "wo") + 1)
                k.did(dve.tensor_tensor(out=pre[:, :, :], in0=pre[:, :, :], in1=fwo[:, :, :], op=ALU.add))
                k.wait()
                dve.wait_ge(stored, 16 * j + 16)
                normalise(k, "x", j, pre, xD, EPS)
                affine(k, xD[:, :, 0:D], g1, be1)
                twice(xD, xD_ready)
                k.end()

            def gate(k, j):
                dve.wait_ge(gate_ready, j + 1)
                k.did(dve.tensor_tensor(out=gl[:, :, :], in0=acc[:, 2 * D:2 * D + 2 * E].rearrange("p (s e) -> p s e", s=2),
                                        in1=bgB[:, None, :].to_broadcast([P, 2, E]), op=ALU.add))
                k.wait()
                k.did(dve.tensor_reduce(gm[:, :], gl[:, :, :], AX.X, ALU.max))
                k.wait()
                dve.tensor_tensor(out=gs[:, :, :], in0=gl[:, :, :], in1=gm[:, :, None].to_broadcast([P, 2, E]),
                                  op=ALU.subtract).then_inc(gate_shift, 1)
                dve.wait_ge(gate_exp, j + 1)
                k.did(dve.tensor_reduce(gsum[:, :], gx[:, :, :], AX.X, ALU.add))
                k.wait()
                k.did(dve.reciprocal(grec[:, :], gsum[:, :]))
                k.wait()
                k.did(dve.tensor_tensor(out=gp[:, :, :], in0=gx[:, :, :], in1=grec[:, :, None].to_broadcast([P, 2, E]),
                                        op=ALU.mult))
                k.wait()
                other = gp[:, :, None, :].to_broadcast([P, 2, E, E])
                own = gp[:, :, :, None].to_broadcast([P, 2, E, E])
                k.did(dve.tensor_tensor(out=ggt[:, :, :, :], in0=other, in1=own, op=ALU.is_gt))
                k.did(dve.tensor_tensor(out=gge[:, :, :, :], in0=other, in1=own, op=ALU.is_equal))
                k.wait()
                k.did(dve.tensor_tensor(out=gge[:, :, :, :], in0=gge[:, :, :, :],
                                        in1=earlier[:, None, :, :].to_broadcast([P, 2, E, E]), op=ALU.mult))
                k.wait()
                k.did(dve.tensor_tensor(out=ggt[:, :, :, :], in0=ggt[:, :, :, :], in1=gge[:, :, :, :], op=ALU.add))
                k.wait()
                k.did(dve.tensor_reduce(grk[:, :, :], ggt[:, :, :, :], AX.X, ALU.add))
                k.wait()
                k.did(dve.scalar_tensor_tensor(out=comb[:, :, :], in0=grk[:, :, :], scalar=1.5, in1=gp[:, :, :],
                                               op0=ALU.is_lt, op1=ALU.mult))
                k.wait()
                for s in range(2):
                    for e in range(E):
                        src = xD[:, s, 0:D] if e == 0 else ff[:, s, :]
                        k.did(dve.scalar_tensor_tensor(out=ff[:, s, :], in0=b2B[:, e, :], scalar=comb[:, s, e:e + 1],
                                                       in1=src, op0=ALU.mult, op1=ALU.add))
                        k.wait()

            def expert_out(k, at, e):
                dve.wait_ge(acc_filled, sum_no(at, f"y{e}") + 1)
                k.did(dve.scalar_tensor_tensor(out=ff[:, 0, :], in0=acc[:, 0:D], scalar=comb[:, 0, e:e + 1],
                                               in1=ff[:, 0, :], op0=ALU.mult, op1=ALU.add))
                dve.scalar_tensor_tensor(out=ff[:, 1, :], in0=acc[:, D:2 * D], scalar=comb[:, 1, e:e + 1],
                                         in1=ff[:, 1, :], op0=ALU.mult, op1=ALU.add).then_inc(acc_drained, 1)
                dve.wait_ge(acc_drained, sum_no(at, f"y{e}") + 1)

            def moe_end(k, j):
                normalise(k, "o", j, ff, res, EPS)
                affine(k, res, g2, be2)
                dve.tensor_tensor(out=res, in0=res, in1=h1keep[:, :, :], op=ALU.add).then_inc(out_ready, 1)

            def ffn_values(at, i):
                dve.wait_ge(drained, drain_no(at, "fval") + 1)
                dve.tensor_tensor(out=fval[:, :, :], in0=fval[:, :, :], in1=over(bvB), op=ALU.add).then_inc(fval_ready, 1)

            def ffn_stats(k, i, strip):
                b = strip % 2
                for s in range(2):
                    u = 2 * strip + s
                    dve.wait_ge(f_scores, FU * i + u + 1)
                    for c in range(FCH):
                        k.did(dve.bn_stats(fst[:, b, FCH * s + c, :], unit_of(u)[:, c, :]))
                    k.did(dve.tensor_reduce(fmax[:, b, FCH * s:FCH * (s + 1)], unit_of(u)[:, 0:FCH, :], AX.X, ALU.max))
                k.wait()

                def stat(n):
                    return fst[:, b, :, n:n + 1].rearrange("p n o -> p (n o)")

                k.did(dve.tensor_tensor(out=fd[:, :], in0=stat(1), in1=stat(4), op=ALU.subtract))
                k.did(dve.tensor_tensor(out=fm2[:, :], in0=stat(2), in1=stat(5), op=ALU.add))
                k.wait()
                k.did(dve.scalar_tensor_tensor(out=fw[:, :], in0=fd[:, :], scalar=T / 4.0, in1=fd[:, :],
                                               op0=ALU.mult, op1=ALU.mult))
                k.wait()
                dve.tensor_tensor(out=fvar[:, b, :], in0=fw[:, :], in1=fm2[:, :], op=ALU.add).then_inc(f_var, 1)

            def ffn_scales(k, i, strip):
                b = strip % 2
                dve.wait_ge(f_sd, 4 * i + strip + 1)
                k.did(dve.tensor_scalar(fden[:, strip, :], fsd[:, b, :], (T - 1.0) ** -0.5, EPS, ALU.mult, ALU.add))
                k.wait()
                k.did(dve.reciprocal(finv[:, strip, :], fden[:, strip, :]))
                k.wait()
                k.did(dve.tensor_scalar(fsc[:, strip, :], finv[:, strip, :], gabs[:, 0:1], None, ALU.mult))
                k.wait()
                dve.scalar_tensor_tensor(out=fnb[:, strip, :], in0=fmax[:, b, :], scalar=-1.0, in1=fsc[:, strip, :],
                                         op0=ALU.mult, op1=ALU.mult).then_inc(f_scale, 1)

            def ffn_turn(i, u):
                dve.wait_ge(f_turned, FU * i + u + 1)
                dve.tensor_copy(probT[:, u % 2, 0:FCH, :], unit_of(u)[:, 0:FCH, :]).then_inc(f_probT, 1)

            def ffn_heads(k, at, i):
                dve.wait_ge(f_exp, FU * FCH * (i + 1))
                k.did(dve.reciprocal(frec[:, :, :], fsum[:, :, :]))
                k.wait()
                dve.wait_ge(acc_filled, sum_no(at, "ffn") + 1)
                dve.tensor_tensor(out=fo[:, :, :].rearrange("p s (h w) -> p (s h) w", w=HD),
                                  in0=acc[:, 0:2 * D].rearrange("p (g w) -> p g w", w=HD),
                                  in1=frec[:, :, :].rearrange("p s h -> p (s h)")[:, :, None].to_broadcast([P, 2 * FHEADS, HD]),
                                  op=ALU.mult).then_inc(acc_drained, 1)

            at = ("first", 0)
            build_onehot(0)
            build_index(at, 0)
            k = Steps(dve, tok_step, 0, 20)
            embed(k, at, 0)
            attn_input(k, 0)
            dve.wait_ge(qv_hi, 1)
            dve.tensor_tensor(out=wqL[:, :], in0=qvA[0], in1=wqH[:, :].bitcast(f32), op=ALU.subtract).then_inc(q_split, 1)
            dve.tensor_tensor(out=wqS[R:P, :], in0=qvB[0], in1=wqS[0:R, :].bitcast(f32), op=ALU.subtract).then_inc(q_split, 1)
            dve.wait_ge(q_split, 2)
            split(at, "aT", aT, aH, aL, a_split, 0)
            dve.wait_ge(ld_small, 16 * SMALL)
            link(dve.tensor_scalar(qscale[:, :], gsc[:, :], 0.0, None, ALU.is_ge))
            link(dve.tensor_scalar(qscale[:, :], qscale[:, :], 2.0, -1.0, ALU.mult, ALU.add))
            link(dve.tensor_tensor(out=gabs[:, :], in0=gsc[:, :], in1=qscale[:, :], op=ALU.mult))
            link(dve.tensor_scalar(qscale[:, :], qscale[:, :], HD ** -0.5, None, ALU.mult))
            link(dve.tensor_scalar(fqb[:, :], fqb[:, :], qscale[:, 0:1], None, ALU.mult))
            dve.wait_ge(drained, drain_no(("first", 0), "fk") + 1)
            for m, (H, L, St) in enumerate(((fqH, fqL, fqS), (fkH, fkL, fkS))):
                def heads(t, rows_):
                    return t[rows_, :].rearrange("p (h w) -> p h w", w=32)[:, :, 0:HD]
                main = fqk[m][:, 0:D].rearrange("p (h w) -> p h w", w=HD)
                rest = fqk[m][0:R, D:2 * D].rearrange("p (h w) -> p h w", w=HD)
                a, r, q = slice(0, P), slice(0, R), slice(R, P)
                link(dve.tensor_copy(heads(H, a), main))
                link(dve.tensor_tensor(out=heads(L, a), in0=main, in1=heads(H, a).bitcast(f32), op=ALU.subtract))
                link(dve.tensor_copy(heads(St, r), rest))
                link(dve.tensor_tensor(out=heads(St, q), in0=rest, in1=heads(St, r).bitcast(f32), op=ALU.subtract))

            def w1_parts(k):
                dve.wait_ge(w1_hi, 2 + k)
                if k == 0:
                    dve.tensor_tensor(out=w1L[:, :], in0=w1A, in1=w1H[:, :].bitcast(f32), op=ALU.subtract)\
                       .then_inc(w1_split, 1)
                c = slice(k * E * FF // 2, (k + 1) * E * FF // 2)
                dve.tensor_tensor(out=w1S[R:P, c], in0=w1B, in1=w1S[0:R, c].bitcast(f32), op=ALU.subtract)\
                   .then_inc(w1_split, 1)

            def step(at, i, full, ahead=True):
                kn = Steps(dve, tok_step, i + 1, 20) if ahead else None
                ka = Steps(dve, attn_step, i, 11)
                kf = Steps(dve, ffn_step, i, 57)
                km = Steps(dve, moe_step, i - 1, 31) if full else None
                if ahead:
                    build_onehot(i + 1)
                if not full:
                    build_index(at, i + 1)
                if full:
                    ffn_tail(at, i - 1)
                    if ahead:
                        build_index(at, i + 1)
                attn_max(i, 0)
                attn_max(i, 1)
                attn_norm(ka, i, 0)
                attn_max(i, 2)
                attn_norm(ka, i, 1)
                attn_max(i, 3)
                attn_turn(i, 0)
                attn_norm(ka, i, 2)
                attn_turn(i, 1)
                attn_norm(ka, i, 3)
                attn_turn(i, 2)
                attn_turn(i, 3)
                if full:
                    split(at, "xT", xT, xH, xL, x_split, i - 1)
                attn_out(ka, at, i)
                if not full:
                    w1_parts(0)
                if full:
                    gate(km, i - 1)
                    if ahead:
                        embed(kn, at, i + 1)
                    expert_out(km, at, 0)
                    if ahead:
                        attn_input(kn, i + 1)
                    expert_out(km, at, 1)
                    dve.wait_ge(drained, drain_no(at, UP[-1]) + 1)
                split(at, "bT", bT, bH, bL, b_split, i)
                if full:
                    expert_out(km, at, 2)
                else:
                    embed(kn, at, i + 1)
                    attn_input(kn, i + 1)
                ffn_values(at, i)
                if ahead:
                    dve.wait_ge(f_scores, FU * i + 1)
                    split(at, "aT", aT, aH, aL, a_split, i + 1)
                ffn_stats(kf, i, 0)
                ffn_stats(kf, i, 1)
                ffn_scales(kf, i, 0)
                ffn_scales(kf, i, 1)
                if full:
                    expert_out(km, at, 3)
                dve.wait_ge(f_scale, 4 * i + 2)
                ffn_turn(i, 0)
                ffn_turn(i, 1)
                ffn_stats(kf, i, 2)
                ffn_turn(i, 2)
                ffn_scales(kf, i, 2)
                ffn_turn(i, 3)
                ffn_stats(kf, i, 3)
                ffn_turn(i, 4)
                ffn_scales(kf, i, 3)
                for u in range(5, FU):
                    ffn_turn(i, u)
                dve.wait_ge(f_scale, 4 * i + 4)
                ffn_heads(kf, at, i)
                dve.wait_ge(acc_drained, sum_no(at, "ffn") + 1)
                dve.sem_inc(fo_ready, 1)
                if full:
                    moe_end(km, i - 1)
                    km.end()
                    dve.wait_ge(out_ready, i)
                if not full:
                    w1_parts(1)
                ka.did(dve.tensor_copy(h1keep[:, :, :], h1[:, :, :]))
                ka.wait()
                ka.end()
                kf.end()

            step(("peel", 0), 0, False)
            with dve.Fori(1, PAIRS - 1, 1) as i:
                step(("loop", i - 1), i, True)
            step(("final", 0), PAIRS - 1, True, ahead=False)
            at = ("last", 0)
            j = PAIRS - 1
            km = Steps(dve, moe_step, j, 31)
            ffn_tail(at, j)
            split(at, "xT", xT, xH, xL, x_split, j)
            gate(km, j)
            for e in range(E):
                expert_out(km, at, e)
            moe_end(km, j)
            km.end()
            one.end()

        @block.tensor
        def _(pe):
            def take(at, name):
                n = drain_no(at, name)
                restarts = DRAIN_START[at[0]] % 3 and DRAINS[at[0]].index(name) == 0
                need = n if restarts else n - 2
                if not isinstance(need, int) or need > 0:
                    pe.wait_ge(drained, need)
                return place(at, name)

            def take_acc(at, name):
                n = sum_no(at, name)
                if not isinstance(n, int) or n > 0:
                    pe.wait_ge(acc_drained, n)

            def mm(dst, lhsT, rhs, start=True, stop=True):
                return pe.matmul(dst, lhsT, rhs, start=start, stop=stop)

            def split_weights(dst, w, c, t):
                H, L, St = w
                hi, lo = t
                mm(dst, H[:, c], hi[:, 0:NT], stop=False)
                mm(dst, H[:, c], lo[:, 0:NT], start=False, stop=False)
                mm(dst, L[:, c], hi[:, 0:NT], start=False, stop=False)
                mm(dst, St[:, c], hi[:, NT:2 * NT], start=False, stop=False)
                return mm(dst, St[:, c], lo[:, NT:2 * NT], start=False)

            def turn(dst, src, n):
                return pe.transpose(dst, src, ident[0:n, 0:n])

            W = ("ids", 0)
            pe.wait_ge(const_ready, 2)
            pe.wait_ge(ids_ready, 1)
            u = take(W, "ids")
            turn(u[0:S, 0:B], ids_f[:, 0, :], B)
            turn(u[0:S, B:2 * B], ids_f[:, 1, :], B).then_inc(filled, 1)
            pe.wait_ge(mask_ready, 1)
            u = take(W, "prefix")
            mm(u[0:S, 0:2 * B], upper[:, :], kmask[:, :, :].rearrange("p a b -> p (a b)")).then_inc(filled, 1)
            pe.wait_ge(ld_tok, 16 * TOK)
            u = take(W, "ke_w")
            turn(u[0:D_ENT, 0:P], kwA[:, :], P)
            turn(u[0:D_ENT, P:D], kwB[:, :], R).then_inc(filled, 1)
            def turn_square(u, A, Bt):
                turn(u[:, 0:P], A[:, 0:P], P)
                turn(u[:, P:D], Bt[:, 0:P], R)
                turn(u[0:R, D:D + P], A[:, P:D], P)
                return turn(u[0:R, D + P:2 * D], Bt[:, P:D], R)

            def index(at, i):
                pe.wait_ge(onehot_ready, i + 1)
                u = take(at, "index")
                mm(u[:, 0:XW], onehot[:, 0, :], embR[:, 0, :])
                mm(u[:, XW:2 * XW], onehot[:, 1, :], embR[:, 1, :]).then_inc(filled, 1)

            def entities(at, i):
                pe.wait_ge(got_ents, 16 * i + 16)
                turn(take(at, "ent")[0:D_ENT, 0:P], entg[:, :], P).then_inc(filled, 1)

            def project_entities(at, i):
                u = take(at, "proj")
                pe.wait_ge(drained, drain_no(at, "ent") + 1)
                mm(u[HALF:P, 0:D], entT[:, 0:HALF], kewT[:, :])
                mm(u[HALF:P, D:2 * D], entT[:, HALF:P], kewT[:, :]).then_inc(filled, 1)

            def turn_tokens(at, name, t, ready, n):
                pe.wait_ge(ready, n + 1)
                u = take(at, name)
                for c in range(2):
                    for s in range(2):
                        ins = turn(u[:, c * NT + s * T:c * NT + (s + 1) * T], t[:, s, c * P:(c + 1) * P], P)
                ins.then_inc(filled, 1)

            def projected_rows(at, m, lo, hi):
                for n in range(lo, hi):
                    u = take(at, (QU, KU)[m][n])
                    for k in range(2):
                        c, dst = 2 * ORDER[n] + k, u[:, k * NT:(k + 1) * NT]
                        cols = slice(c * P, (c + 1) * P)
                        if m == 0:
                            ins = split_weights(dst, (wqH, wqL, wqS), cols, (aH, aL))
                            continue
                        h, w = divmod(c, QCH // 2)
                        r = slice(R * h, R * h + R)
                        mm(dst, wk[:, cols], aT[:, 0:NT], stop=False)
                        ins = mm(dst, wkR[r, w * P:(w + 1) * P], aT[r, NT:2 * NT], start=False)
                    ins.then_inc(filled, 1)

            def values(at, n):
                s, c = n // 3, slice(n % 3 * 512, (n % 3 + 1) * 512)
                u = take(at, VU[n])
                m, r = slice(s * T, (s + 1) * T), slice(NT + s * T, NT + (s + 1) * T)
                mm(u[:, :], aH[:, m], wvH[:, c], stop=False)
                mm(u[:, :], aH[:, m], wvL[:, c], start=False, stop=False)
                mm(u[:, :], aL[:, m], wvH[:, c], start=False, stop=False)
                mm(u[:, :], aH[:, r], wvS[:, c], start=False, stop=False)
                mm(u[:, :], aL[:, r], wvS[:, c], start=False).then_inc(filled, 1)

            def attn_scores(at, i, u):
                s = u // 2
                if u == 0:
                    pe.wait_ge(drained, drain_no(at, KU[-1]) + 1)
                r = slice(R * s, R * s + R)
                for k in range(4):
                    g = 4 * u + k
                    m = slice(g * T, (g + 1) * T)
                    n = slice(NM + (g - s * HEADS) * T, NM + (g - s * HEADS + 1) * T)
                    mm(unit_of(u)[:, k, :], qt[:, m], kt[:, m], stop=False)
                    ins = mm(unit_of(u)[:, k, :], qt[r, n], kt[r, n], start=False)
                ins.then_inc(a_scores, 1)

            def attn_turn(i, u):
                pe.wait_ge(a_prob, 4 * i + u + 1)
                for k in range(4):
                    ins = turn(unit_of(u)[:, k, :], prob[:, u, k, :], P)
                ins.then_inc(a_turned, 1)

            def attn_values(at, i, u):
                s = u // 2
                if u % 2 == 0:
                    pe.wait_ge(v_ready, 2 * i + s + 1)
                pe.wait_ge(a_probT, 4 * i + u + 1)
                main = take(at, f"om{u}")
                for k in range(4):
                    ins = mm(main[:, k * T:(k + 1) * T], v2[s][:, u % 2 * 4 + k, 0:P], probT[:, u % 2, k, :])
                ins.then_inc(filled, 1)
                rest = take(at, f"or{s}") if u % 2 == 0 else place(at, f"or{s}")
                for k in range(4):
                    w = T // 2
                    c = (u % 2 * 4 + k) * w
                    for j in range(2):
                        ins = mm(rest[R * j:R * j + R, c:c + w], v2[s][:, u % 2 * 4 + k, P:D],
                                 probT[:, u % 2, k, :].rearrange("p (n j) -> p j n", j=2)[:, j, :])
                if u % 2:
                    ins.then_inc(filled, 1)

            def attn_out(at, s):
                if s == 0:
                    take_acc(at, "attn")
                pe.wait_ge(drained, drain_no(at, f"or{s}") + 1)
                t, dst = slice(s * T, (s + 1) * T), acc[:, s * D:(s + 1) * D]
                for c in range(HEADS):
                    mm(dst, oT[:, c, t], wp[:, c, :], start=c == 0, stop=False)
                for p in range(HP):
                    ins = mm(dst, oR[:, p, t], wpR[:, p, :], start=False, stop=p == HP - 1)
                if s == 1:
                    ins.then_inc(acc_filled, 1)

            def turn_heads(at, j):
                pe.wait_ge(fo_ready, j + 1)
                u = take(at, "attnT")
                for s in range(2):
                    turn(u[:, s * T:(s + 1) * T], fo[:, s, 0:P], P)
                    ins = turn(u[0:R, NT + s * T:NT + (s + 1) * T], fo[:, s, P:D], P)
                ins.then_inc(filled, 1)

            def out_projection(at):
                u = take(at, "wo")
                pe.wait_ge(drained, drain_no(at, "attnT") + 1)
                for s in range(2):
                    t = slice(s * T, (s + 1) * T)
                    mm(u[:, s * D:(s + 1) * D], foT[:, 0, t], fvo[:, 1, 0:D], stop=False)
                    ins = mm(u[:, s * D:(s + 1) * D], foT[0:R, 1, t], fvo[0:R, 1, D:2 * D], start=False)
                ins.then_inc(filled, 1)

            def gate(at, j):
                take_acc(at, "y0")
                for s in range(2):
                    dst = acc[:, 2 * D + s * E:2 * D + (s + 1) * E]
                    mm(dst, xT[:, s * T:(s + 1) * T], wgT[:, 0:E], stop=False)
                    ins = mm(dst, xT[0:R, NT + s * T:NT + (s + 1) * T], wgT[0:R, E:2 * E], start=False)
                ins.then_inc(gate_ready, 1)

            def expert_up(at, e):
                for n in range(e * KCH // 2, (e + 1) * KCH // 2):
                    u = take(at, UP[n])
                    for k in range(2):
                        c = 2 * n + k
                        ins = split_weights(u[:, k * NT:(k + 1) * NT], (w1H, w1L, w1S), slice(c * P, (c + 1) * P), (xH, xL))
                    ins.then_inc(filled, 1)

            def expert_down(at, j, e):
                take_acc(at, f"y{e}")
                if e == 0:
                    pe.wait_ge(ld_w2, 16)
                    pe.wait_ge(gate_shift, j + 1)
                pe.wait_ge(drained, drain_no(at, UP[(e + 1) * KCH // 2 - 1]) + 1)
                for s in range(2):
                    for k in range(KCH):
                        ins = mm(acc[:, s * D:(s + 1) * D], hid[:, e % 2, k, s * T:(s + 1) * T], w2[:, e * KCH + k, :],
                                 start=k == 0, stop=k == KCH - 1)
                ins.then_inc(acc_filled, 1)

            def ffn_projection(at, c):
                u = take(at, f"qk{c}")
                w = slice(c * P, (c + 1) * P)
                split_weights(u[:, 0:NT], (fqH, fqL, fqS), w, (bH, bL))
                split_weights(u[:, NT:2 * NT], (fkH, fkL, fkS), w, (bH, bL)).then_inc(filled, 1)

            def ffn_value(at):
                u = take(at, "fval")
                pe.wait_ge(drained, drain_no(at, "bT") + 1)
                for s in range(2):
                    mm(u[:, s * D:(s + 1) * D], bT[:, s * T:(s + 1) * T], fvo[:, 0, 0:D], stop=False)
                    ins = mm(u[:, s * D:(s + 1) * D], bT[0:R, NT + s * T:NT + (s + 1) * T], fvo[0:R, 0, D:2 * D], start=False)
                ins.then_inc(filled, 1)

            def ffn_scores(at, i, u):
                k, s = u // 2, u % 2
                if u == 0:
                    pe.wait_ge(drained, drain_no(at, "qk2") + 1)
                r, t = slice(32 * k, 32 * k + 32), slice(s * T, (s + 1) * T)
                for c in range(FCH):
                    ins = mm(unit_of(u)[:, c, :], fqT[r, c, t], fkT[r, c, t])
                ins.then_inc(f_scores, 1)

            def ffn_turn(i, u):
                pe.wait_ge(f_exp, FU * FCH * i + FCH * (u + 1))
                for c in range(FCH):
                    ins = turn(unit_of(u)[:, c, :], prob[:, u % 4, c, :], P)
                ins.then_inc(f_turned, 1)

            def ffn_values(at, i, u):
                k, s = u // 2, u % 2
                if u == 0:
                    take_acc(at, "ffn")
                    pe.wait_ge(fval_ready, i + 1)
                pe.wait_ge(f_probT, FU * i + u + 1)
                for c in range(FCH):
                    h = 4 * c + k
                    ins = mm(acc[:, s * D + h * HD:s * D + (h + 1) * HD], probT[:, u % 2, c, :], fval[:, s, h * HD:(h + 1) * HD])
                if u == FU - 1:
                    ins.then_inc(acc_filled, 1)

            at = ("first", 0)
            index(at, 0)
            entities(at, 0)
            project_entities(at, 0)
            pe.wait_ge(ld_rows, 16 * ROWS)
            u, nb = take(at, "small"), 2 * QCH
            turn(u[:, 0:nb], b1row[:, :], E * KCH)
            turn(u[:, nb:2 * nb], brow[:, :], nb)
            turn(u[:, 2 * nb:2 * nb + E], wgrow[:, 0:P], E)
            turn(u[0:R, 2 * nb + E:2 * nb + 2 * E], wgrow[:, P:D], E).then_inc(filled, 1)
            turn_tokens(at, "aT", aD, aD_ready, 0)
            pe.wait_ge(q_split, 2)
            pe.wait_ge(a_split, 2)
            projected_rows(at, 0, 0, 6)
            pe.wait_ge(v_split, 2)
            for n in range(6):
                values(at, n)
            pe.wait_ge(ld_small, 16 * SMALL)
            for m, name in enumerate(("fq", "fk", "fv", "fo")):
                c = m * 2 * D
                turn_square(take(at, name), fstage[:, c:c + D], fstage[0:R, c + D:c + 2 * D]).then_inc(filled, 1)
            pe.wait_ge(ld_attn, 16 * 12)

            def step(at, i, full, ahead=True):
                projected_rows(at, 1, 0, 1)
                if full:
                    turn_heads(at, i - 1)
                projected_rows(at, 1, 1, 3)
                if full:
                    out_projection(at)
                else:
                    index(at, i + 1)
                projected_rows(at, 1, 3, 6)
                if full and ahead:
                    index(at, i + 1)
                for u in range(4):
                    attn_scores(at, i, u)
                attn_turn(i, 0)
                attn_turn(i, 1)
                attn_values(at, i, 0)
                attn_turn(i, 2)
                attn_values(at, i, 1)
                attn_turn(i, 3)
                attn_values(at, i, 2)
                attn_values(at, i, 3)
                attn_out(at, 0)
                if full:
                    turn_tokens(at, "xT", xD, xD_ready, i - 1)
                attn_out(at, 1)
                if ahead:
                    entities(at, i + 1)
                if full:
                    pe.wait_ge(x_split, 2 * (i - 1) + 2)
                    pe.wait_ge(w1_split, 3)
                    expert_up(at, 0)
                    gate(at, i - 1)
                    if ahead:
                        project_entities(at, i + 1)
                    expert_up(at, 1)
                    expert_down(at, i - 1, 0)
                turn_tokens(at, "bT", bD, bD_ready, i)
                if full:
                    expert_up(at, 2)
                    ffn_value(at)
                    expert_down(at, i - 1, 1)
                    expert_up(at, 3)
                    expert_down(at, i - 1, 2)
                else:
                    project_entities(at, i + 1)
                    ffn_value(at)
                pe.wait_ge(b_split, 2 * i + 2)
                for c in range(FCH):
                    ffn_projection(at, c)
                if full and ahead:
                    turn_tokens(at, "aT", aD, aD_ready, i + 1)
                for u in range(4):
                    ffn_scores(at, i, u)
                if full:
                    expert_down(at, i - 1, 3)
                if ahead:
                    if not full:
                        turn_tokens(at, "aT", aD, aD_ready, i + 1)
                    pe.wait_ge(a_split, 2 * (i + 1) + 2)
                    projected_rows(at, 0, 0, 4)
                ffn_turn(i, 0)
                ffn_turn(i, 1)
                ffn_values(at, i, 0)
                ffn_scores(at, i, 4)
                if ahead:
                    projected_rows(at, 0, 4, 5)
                ffn_values(at, i, 1)
                ffn_scores(at, i, 5)
                ffn_turn(i, 2)
                ffn_turn(i, 3)
                if ahead:
                    projected_rows(at, 0, 5, 6)
                ffn_values(at, i, 2)
                ffn_scores(at, i, 6)
                if ahead:
                    values(at, 0)
                ffn_values(at, i, 3)
                ffn_scores(at, i, 7)
                if ahead:
                    values(at, 1)
                ffn_turn(i, 4)
                ffn_turn(i, 5)
                if ahead:
                    values(at, 2)
                ffn_values(at, i, 4)
                if ahead:
                    values(at, 3)
                ffn_values(at, i, 5)
                if ahead:
                    values(at, 4)
                ffn_turn(i, 6)
                ffn_turn(i, 7)
                if ahead:
                    values(at, 5)
                ffn_values(at, i, 6)
                ffn_values(at, i, 7)

            step(("peel", 0), 0, False)
            with pe.Fori(1, PAIRS - 1, 1) as i:
                step(("loop", i - 1), i, True)
            step(("final", 0), PAIRS - 1, True, ahead=False)
            at = ("last", 0)
            j = PAIRS - 1
            turn_heads(at, j)
            out_projection(at)
            turn_tokens(at, "xT", xD, xD_ready, j)
            pe.wait_ge(x_split, 2 * j + 2)
            gate(at, j)
            expert_up(at, 0)
            expert_up(at, 1)
            expert_down(at, j, 0)
            expert_up(at, 2)
            expert_down(at, j, 1)
            expert_up(at, 3)
            expert_down(at, j, 2)
            expert_down(at, j, 3)


_INS = ["x", "mask_BS_i0_1"] + [f"L0_tok_{n}" for n in (
    "word_emb", "pos_emb", "tt_emb", "entityVec", "ke_w", "ke_b", "w_gamma", "w_beta", "k_gamma", "k_beta")] + [
    f"L0_attn_{n}" for n in ("W_qkv", "b_qkv", "W_proj", "b_proj")] + [
    f"L0_ffn_{n}" for n in ("Wq", "bq", "Wk", "bk", "Wv", "bv", "Wo", "bo", "gamma", "ln1_g", "ln1_b", "ln2_g",
                            "ln2_b", "Wg", "bg", "W1", "b1", "W2", "b2")]


def kernel(**inputs):
    import numpy as _np
    import concourse.bacc as _bacc
    from concourse import mybir as _mybir
    from concourse.bass_utils import run_bass_kernel_spmd as _run

    nc = _bacc.Bacc("TRN2", target_bir_lowering=False, num_devices=1, dynamic_dma_scratch_size=4096)
    arrays, args = {}, []
    for name in _INS:
        a = _np.ascontiguousarray(inputs[name])
        if a.ndim == 0:
            a = a.reshape(1)
        arrays[f"in_{name}_dram"] = a
        args.append(nc.dram_tensor(f"in_{name}_dram", a.shape, _mybir.dt.from_np(a.dtype), kind="ExternalInput").ap())
    args.append(nc.dram_tensor("out_0_dram", (B, T, D), _mybir.dt.float32, kind="ExternalOutput").ap())
    lm_tower_kernel(nc, *args)
    r = _run(nc, [arrays], core_ids=[0])
    return r.results[0]["out_0_dram"]
```
